# Optimizing a Trainium2 kernel written in Bass

```python
import numpy as np
import jax
import jax.numpy as jnp

def _softmax(x, axis=-1):
    return jax.nn.softmax(x, axis=axis)

def _gelu(x):
    return jax.nn.gelu(x, approximate=True)

def _silu(x):
    return jax.nn.silu(x)

def _sigmoid(x):
    return jax.nn.sigmoid(x)

def _layernorm(x, axis=-1, eps=1e-05):
    m = jnp.mean(x, axis=axis, keepdims=True)
    v = jnp.var(x, axis=axis, keepdims=True)
    return (x - m) / jnp.sqrt(v + eps)

def _scatter_add(tgt, idx, src, axis=0):
    return tgt.at[idx].add(src)

def _segment_sum(src, seg, n):
    return jax.ops.segment_sum(src, seg, n)
kernel_name = 'mk_sandwich_d1_jaxref_r4_695eff'

def setup_inputs(seed: int=0):
    np.random.seed(seed)
    _w = jnp.asarray

    def _L0_attn_setup():
        import jax, jax.numpy as jnp
        import numpy as np
        EMBED = 256
        HEADS = 16
        key = jax.random.key(seed)
        ks = jax.random.split(key, 6)
        N, S = (1, 1024)
        half = EMBED // 2
        x = jax.random.normal(ks[0], (N, S, EMBED), dtype=jnp.float32)
        Wq = jax.random.normal(ks[1], (half, half), dtype=jnp.float32) * 0.02
        Wk = jax.random.normal(ks[2], (half, half), dtype=jnp.float32) * 0.02
        Wv = jax.random.normal(ks[3], (half, half), dtype=jnp.float32) * 0.02
        Wo = jax.random.normal(ks[4], (EMBED, half), dtype=jnp.float32) * 0.02
        bo = jnp.zeros((EMBED,), dtype=jnp.float32)
        return {'x': x, 'Wq': Wq, 'Wk': Wk, 'Wv': Wv, 'Wo': Wo, 'bo': bo}
    _L0_attn_in = _L0_attn_setup()

    def _L0_ffn_setup():
        import jax, jax.numpy as jnp
        import numpy as np
        B, S, DIM = (4, 1024, 256)
        BASE_COUPLING = 0.1
        NUM_CYCLES = 3

        def _gelu(x):
            return jax.nn.gelu(x, approximate=False)

        def _coupling_net(h, w1, b1, w2, b2, w3, b3, w4, b4):
            h = _gelu(h @ w1 + b1)
            h = _gelu(h @ w2 + b2)
            h = _gelu(h @ w3 + b3)
            return jax.nn.sigmoid(h @ w4 + b4)

        def _global_net(h, w1, b1, w2, b2, w3, b3):
            h = _gelu(h @ w1 + b1)
            h = _gelu(h @ w2 + b2)
            return jax.nn.sigmoid(h @ w3 + b3)

        def _twist(x):
            o_r, o_i, p_r, p_i = jnp.split(x, 4, axis=-1)
            return jnp.concatenate([p_r, -p_i, -o_r, o_i], axis=-1)
        key = jax.random.key(seed)
        ks = jax.random.split(key, 9)
        d = DIM

        def w(k, fan_in, fan_out):
            return jax.random.normal(k, (fan_in, fan_out), dtype=jnp.float32) / np.sqrt(fan_in).astype(np.float32)
        inp = {'x': jax.random.normal(ks[0], (B, S, d), dtype=jnp.float32)}
        cn_dims = [(d, d), (d, d // 2), (d // 2, d // 4), (d // 4, 1)]
        for i, (a, b) in enumerate(cn_dims):
            inp[f'cn_w{i + 1}'] = w(ks[1 + i], a, b)
            inp[f'cn_b{i + 1}'] = jnp.zeros((b,), dtype=jnp.float32)
        gc_dims = [(d, d // 2), (d // 2, d // 4), (d // 4, 1)]
        for i, (a, b) in enumerate(gc_dims):
            inp[f'gc_w{i + 1}'] = w(ks[5 + i], a, b)
            inp[f'gc_b{i + 1}'] = jnp.zeros((b,), dtype=jnp.float32)
        inp['adaptive_range'] = jnp.full((1,), 0.2, dtype=jnp.float32)
        return inp
    _L0_ffn_in = _L0_ffn_setup()
    _d = {'L0_attn_x': _L0_attn_in['x'], 'L0_attn_Wq': _L0_attn_in['Wq'], 'L0_attn_Wk': _L0_attn_in['Wk'], 'L0_attn_Wv': _L0_attn_in['Wv'], 'L0_attn_Wo': _L0_attn_in['Wo'], 'L0_attn_bo': _L0_attn_in['bo'], 'L0_ffn_cn_w1': _L0_ffn_in['cn_w1'], 'L0_ffn_cn_b1': _L0_ffn_in['cn_b1'], 'L0_ffn_cn_w2': _L0_ffn_in['cn_w2'], 'L0_ffn_cn_b2': _L0_ffn_in['cn_b2'], 'L0_ffn_cn_w3': _L0_ffn_in['cn_w3'], 'L0_ffn_cn_b3': _L0_ffn_in['cn_b3'], 'L0_ffn_cn_w4': _L0_ffn_in['cn_w4'], 'L0_ffn_cn_b4': _L0_ffn_in['cn_b4'], 'L0_ffn_gc_w1': _L0_ffn_in['gc_w1'], 'L0_ffn_gc_b1': _L0_ffn_in['gc_b1'], 'L0_ffn_gc_w2': _L0_ffn_in['gc_w2'], 'L0_ffn_gc_b2': _L0_ffn_in['gc_b2'], 'L0_ffn_gc_w3': _L0_ffn_in['gc_w3'], 'L0_ffn_gc_b3': _L0_ffn_in['gc_b3'], 'L0_ffn_adaptive_range': _L0_ffn_in['adaptive_range']}
    _x0 = _d['L0_attn_x']
    _d['L0_attn_x'] = jax.random.normal(jax.random.fold_in(jax.random.key(seed), 1), (16, 1024, 256), dtype=_x0.dtype)
    del _x0
    return _d

def reference(L0_attn_x, L0_attn_Wq, L0_attn_Wk, L0_attn_Wv, L0_attn_Wo, L0_attn_bo, L0_ffn_cn_w1, L0_ffn_cn_b1, L0_ffn_cn_w2, L0_ffn_cn_b2, L0_ffn_cn_w3, L0_ffn_cn_b3, L0_ffn_cn_w4, L0_ffn_cn_b4, L0_ffn_gc_w1, L0_ffn_gc_b1, L0_ffn_gc_w2, L0_ffn_gc_b2, L0_ffn_gc_w3, L0_ffn_gc_b3, L0_ffn_adaptive_range):

    def _L0_attn_ref(x, Wq, Wk, Wv, Wo, bo):
        import jax, jax.numpy as jnp
        import numpy as np
        EMBED = 256
        HEADS = 16
        N, S, E = x.shape
        H = HEADS
        Dh = E // 2 // H
        scale = float(E // H) ** 0.5
        left = x[..., :E // 2]
        q = (left @ Wq.T).reshape(N, S, H, Dh)
        k = (left @ Wk.T).reshape(N, S, H, Dh)
        v = (left @ Wv.T).reshape(N, S, H, Dh)
        energy = jnp.einsum('nqhd,nkhd->nqkh', q, k)
        att = jax.nn.softmax(energy / scale, axis=2)
        out = jnp.einsum('nqkh,nkhd->nqhd', att, v)
        out = out.reshape(N, S, E // 2)
        return out @ Wo.T + bo

    def _L0_ffn_ref(x, cn_w1, cn_b1, cn_w2, cn_b2, cn_w3, cn_b3, cn_w4, cn_b4, gc_w1, gc_b1, gc_w2, gc_b2, gc_w3, gc_b3, adaptive_range):
        import jax, jax.numpy as jnp
        import numpy as np
        B, S, DIM = (4, 1024, 256)
        BASE_COUPLING = 0.1
        NUM_CYCLES = 3

        def _gelu(x):
            return jax.nn.gelu(x, approximate=False)

        def _coupling_net(h, w1, b1, w2, b2, w3, b3, w4, b4):
            h = _gelu(h @ w1 + b1)
            h = _gelu(h @ w2 + b2)
            h = _gelu(h @ w3 + b3)
            return jax.nn.sigmoid(h @ w4 + b4)

        def _global_net(h, w1, b1, w2, b2, w3, b3):
            h = _gelu(h @ w1 + b1)
            h = _gelu(h @ w2 + b2)
            return jax.nn.sigmoid(h @ w3 + b3)

        def _twist(x):
            o_r, o_i, p_r, p_i = jnp.split(x, 4, axis=-1)
            return jnp.concatenate([p_r, -p_i, -o_r, o_i], axis=-1)
        global_context = x.mean(axis=1, keepdims=True)
        gf = _global_net(global_context, gc_w1, gc_b1, gc_w2, gc_b2, gc_w3, gc_b3)
        out = x
        for _ in range(NUM_CYCLES):
            tf = _coupling_net(out, cn_w1, cn_b1, cn_w2, cn_b2, cn_w3, cn_b3, cn_w4, cn_b4)
            combined = 0.7 * gf + 0.3 * tf
            coupling = BASE_COUPLING + adaptive_range * (combined - 0.5) * 2.0
            out = out + coupling * _twist(out)
        return out
    x = L0_attn_x
    x = x + _layernorm(_L0_attn_ref(_layernorm(x, axis=-1), L0_attn_Wq, L0_attn_Wk, L0_attn_Wv, L0_attn_Wo, L0_attn_bo), axis=-1)
    x = x + _layernorm(_L0_ffn_ref(_layernorm(x, axis=-1), L0_ffn_cn_w1, L0_ffn_cn_b1, L0_ffn_cn_w2, L0_ffn_cn_b2, L0_ffn_cn_w3, L0_ffn_cn_b3, L0_ffn_cn_w4, L0_ffn_cn_b4, L0_ffn_gc_w1, L0_ffn_gc_b1, L0_ffn_gc_w2, L0_ffn_gc_b2, L0_ffn_gc_w3, L0_ffn_gc_b3, L0_ffn_adaptive_range), axis=-1)
    return x

_drawn_inputs = setup_inputs


def setup_inputs(seed=0):
    import zlib

    import numpy as np

    out = dict(_drawn_inputs(seed))
    spreads = {'L0_attn_bo': (0.0, 0.1),
     'L0_ffn_cn_b1': (0.0, 0.8),
     'L0_ffn_cn_b2': (0.0, 0.8),
     'L0_ffn_cn_b3': (0.0, 0.8),
     'L0_ffn_gc_b1': (0.0, 0.8),
     'L0_ffn_gc_b2': (0.0, 0.8)}
    factors = {'L0_attn_Wq': 8.0,
     'L0_attn_Wk': 8.0,
     'L0_attn_Wv': 4.826,
     'L0_attn_Wo': 4.747,
     'L0_ffn_cn_w1': 6.159,
     'L0_ffn_cn_w2': 8.0,
     'L0_ffn_cn_w3': 8.0,
     'L0_ffn_cn_w4': 6.708,
     'L0_ffn_gc_w1': 3.747,
     'L0_ffn_gc_w2': 8.0,
     'L0_ffn_gc_w3': 6.795}
    for name, (base, spread) in spreads.items():
        noise = np.random.default_rng([zlib.crc32(name.encode()), seed]).standard_normal(out[name].shape)
        drawn = base * np.exp(spread * noise) if base else spread * noise
        out[name] = jnp.asarray(drawn.astype(out[name].dtype))
    for name, factor in factors.items():
        out[name] = (out[name] * factor).astype(out[name].dtype)
    return out
```

```python
from contextlib import ExitStack

import concourse.bass as bass
from concourse import mybir

F32 = mybir.dt.float32
BF16 = mybir.dt.bfloat16
ACT = mybir.ActivationFunctionType
ALU = mybir.AluOpType
AX = mybir.AxisListType

P = 128
BANK = 512
EPS = 1e-5
TERMS = [(0, 0), (0, 1), (0, 2), (1, 0), (1, 1), (2, 0)]


class Queue:

    def __init__(self):
        self.items, self.seen = [], {}

    def wait(self, *marks):
        for mark in marks:
            if mark is None:
                continue
            sem, value = mark
            if self.seen.get(id(sem), 0) < value:
                self.seen[id(sem)] = value
                self.items.append(lambda e, s=sem.sem, v=value: e.wait_ge(s, v))

    def do(self, emit, sem=None, by=1):
        if sem is None:
            self.items.append(emit)
            return None
        sem.value += by
        self.items.append(lambda e: emit(e).then_inc(sem.sem, by))
        return (sem, sem.value)


class Counter:

    def __init__(self, sem):
        self.sem, self.value = sem, 0


def attention_ffn_program(nc, a):
    N, S, E = a["x"].shape
    D = E // 2
    H = 16
    DH = D // H
    HP = H // 2
    NT = S // P
    NH = S // BANK
    TPH = BANK // P
    NG = H // 4
    ROWS = DH * len(TERMS)
    MROWS = 3
    SCALE = 1.0 / float(E // H) ** 0.5
    assert (S, E, DH, NH) == (1024, 256, 8, 2)

    x_dram = a["x"].rearrange("n (p t) e -> n p t e", p=P)
    out_dram = a["out"].rearrange("n (p t) e -> n p t e", p=P)

    with ExitStack() as ctx:
        def sb(name, shape, dt=F32):
            return ctx.enter_context(nc.sbuf_tensor(name, shape, dt))

        def counter(name):
            return Counter(ctx.enter_context(nc.semaphore(name)))

        scoresT_ps = ctx.enter_context(nc.psum_tensor("scoresT_ps", [P, 4 * BANK], F32))
        max_ps = ctx.enter_context(nc.psum_tensor("max_ps", [P, 2 * BANK], F32))
        heads_ps = ctx.enter_context(nc.psum_tensor("heads_ps", [P, BANK], F32))
        misc_ps = ctx.enter_context(nc.psum_tensor("misc_ps", [P, BANK], F32))

        XS = 5
        x_sb = sb("x_sb", [P, XS, NT, E])
        q_rows = sb("q_rows", [P, 2, HP, S], BF16)
        k_rows = sb("k_rows", [P, 2, HP, S], BF16)
        v_sb = sb("v_sb", [P, 2, NT, H, DH + 2])
        NP = 3
        p_sb = sb("p_sb", [P, NP, 4, BANK])
        headsT = sb("headsT", [P, NH, NG, BANK])
        parts = sb("parts", [P, 2, 3, S], BF16)
        tok = sb("tok", [P, NT, D])
        feat = sb("feat", [P, S])
        y_sb = sb("y_sb", [P, NT, E])
        y_flat = y_sb[:, :, :].rearrange("p t e -> p (t e)")
        proj_sb, rest_sb = y_flat[:, 0:BANK], y_flat[:, BANK:2 * BANK]
        state = sb("state", [P, 2, S])
        wq, wk, wv = sb("wq", [P, D]), sb("wk", [P, D]), sb("wv", [P, D])
        wo = sb("wo", [P, E])
        bo = sb("bo", [P, E])
        w1, w2, w3 = sb("w1", [P, 2, E]), sb("w2", [P, 2, D]), sb("w3", [P, D // 2])
        g1, g2 = sb("g1", [P, 2, D]), sb("g2", [P, D // 2])
        b1, b2, b3 = sb("b1", [P, 2]), sb("b2", [P, 1]), sb("b3", [D // 2, 1])
        gb1, gb2 = sb("gb1", [P, 1]), sb("gb2", [D // 2, 1])
        w4, g3 = sb("w4", [D // 2, 1]), sb("g3", [D // 2, 1])
        w4_all, g3_all = sb("w4_all", [D // 2, P]), sb("g3_all", [D // 2, P])
        b4, gb3, ar = sb("b4", [P, 1]), sb("gb3", [P, 1]), sb("ar", [P, 1])
        b4_half, gb3_half = sb("b4_half", [P, 1]), sb("gb3_half", [P, 1])
        ones = sb("ones", [D // 2, P])
        ident = sb("ident", [P, P])
        sign = sb("sign", [P, 1])
        tenth = sb("tenth", [P, 1])
        ar_token = sb("ar_token", [P, 1])
        ar_global = sb("ar_global", [P, 1])
        shift = sb("shift", [P, 1])
        max_parts = sb("max_parts", [P, 2, P])
        max_all = sb("max_all", [P, P])
        neg_max = sb("neg_max", [P, P])
        neg_rest = sb("neg_rest", [P, P])
        neg_parts = sb("neg_parts", [P, 3, P], BF16)
        stats = sb("stats", [P, NT, 6])
        moments = sb("moments", [P, NT, 2])
        rstd = sb("rstd", [P, NT])
        minus_half = sb("minus_half", [P, NT])
        recip = sb("recip", [P, H])
        sums = sb("sums", [P, 2, NH])
        mean_g = sb("mean_g", [P, 2])
        hg1, hg2, tg = sb("hg1", [P, 1]), sb("hg2", [D // 2, 1]), sb("tg", [P, 1])

        c_w = counter("weights_loaded")
        c_x = [counter(f"x_loaded{i}") for i in range(XS)]
        c_out = [counter(f"out_stored{i}") for i in range(XS)]
        c_rows = [counter(f"rows_laid{i}") for i in range(2)]
        c_mrows = [counter(f"max_rows_laid{i}") for i in range(2)]
        c_set = counter("constants_set")
        c_set_p = counter("constants_pool")
        c_st = counter("scoresT_done")
        c_pv = counter("pv_done")
        c_mm = counter("max_scores_done")
        c_mi = counter("misc_mm_done")
        c_ff = counter("ffn_mm_done")
        c_exp = counter("exp_done")
        c_act = counter("act_misc_done")
        c_red = counter("max_taken")
        c_dve = counter("dve_misc_done")
        c_pool = counter("pool_done")

        pe, act, dve, pool, sp = Queue(), Queue(), Queue(), Queue(), Queue()

        def load(dst, src):
            return sp.do(lambda e: e.dma_start(dst, src), c_w, 16)

        def load_x(b):
            slot = b % XS
            if b >= XS:
                sp.wait(stored[b - XS])
            loaded[b] = sp.do(lambda e: e.dma_start(x_sb[:, slot, :, :], x_dram[b]), c_x[slot], 16)

        loaded, stored = {}, {}
        load_x(0)
        load(wq[:, :], a["wq_t"])
        load(wk[:, :], a["wk_t"])
        load(wv[:, :], a["wv_t"])
        load(wo[:, :], a["wo_t"])
        load(bo[:, :], a["bo"].partition_broadcast(P))
        load(w1[:, :, :], a["w1"].rearrange("(k p) n -> p k n", p=P))
        load(w2[:, :, :], a["w2"].rearrange("(k p) n -> p k n", p=P))
        load(w3[:, :], a["w3"])
        load(w4[:, :], a["w4"])
        load(g1[:, :, :], a["g1"].rearrange("(k p) n -> p k n", p=P))
        load(g2[:, :], a["g2"])
        load(g3[:, :], a["g3"])
        for k in range(2):
            load(b1[:, k:k + 1], a["b1"][k * P:(k + 1) * P].rearrange("(p k) -> p k", k=1))
        load(b2[:, :], a["b2"].rearrange("(p k) -> p k", k=1))
        load(b3[:, :], a["b3"].rearrange("(p k) -> p k", k=1))
        load(gb1[:, :], a["gb1"].rearrange("(p k) -> p k", k=1))
        load(gb2[:, :], a["gb2"].rearrange("(p k) -> p k", k=1))
        load(b4[:, :], a["b4"].partition_broadcast(P))
        load(gb3[:, :], a["gb3"].partition_broadcast(P))
        weights = load(ar[:, :], a["ar"].partition_broadcast(P))
        for b in range(1, min(2, N)):
            load_x(b)

        id0 = pool.do(lambda e: e.memset(ident[:, :], 0.0), c_set_p)
        pool.wait(id0)
        ident_set = pool.do(lambda e: e.affine_select(
            out=ident[:, :], in_=ident[:, :], compare_op=ALU.not_equal, fill=1.0, base=0,
            pattern=[[-1, P]], channel_multiplier=1), c_set_p)

        dve.do(lambda e: e.memset(heads_ps[:, :], 0.0))
        dve.do(lambda e: e.memset(v_sb[:, :, :, :, :], 1.0))
        dve.do(lambda e: e.memset(minus_half[:, :], -0.5))
        dve.do(lambda e: e.memset(sign[0:D // 2, :], 1.0))
        dve.do(lambda e: e.memset(sign[D // 2:D, :], -1.0))
        for side in range(2):
            dve.do(lambda e, s=side: e.memset(k_rows[64 * s + 32:64 * s + 64, :, :, :], 1.0))
        const_set = dve.do(lambda e: e.memset(ones[:, :], 1.0), c_set)
        dve.wait(const_set, weights)
        dve.do(lambda e: e.tensor_scalar(w4_all[:, :], ones[:, :], w4[:, 0:1], None, ALU.mult))
        dve.do(lambda e: e.tensor_scalar(g3_all[:, :], ones[:, :], g3[:, 0:1], None, ALU.mult))
        dve.do(lambda e: e.tensor_scalar(b4_half[:, :], b4[:, :], 0.5, None, ALU.mult))
        dve.do(lambda e: e.tensor_scalar(gb3_half[:, :], gb3[:, :], 0.5, None, ALU.mult))
        dve.do(lambda e: e.tensor_scalar(tenth[:, :], sign[:, :], 0.1, None, ALU.mult))
        dve.do(lambda e: e.tensor_scalar(ar_token[:, :], sign[:, :], ar[:, 0:1], 0.3, ALU.mult, ALU.mult))
        derived = dve.do(lambda e: e.tensor_scalar(ar_global[:, :], sign[:, :], ar[:, 0:1], 0.7,
                                                   ALU.mult, ALU.mult), c_set)
        pe.wait(ident_set, weights, const_set, derived)
        act.wait(weights, derived)
        pool.wait(derived)
        sp.wait(const_set)

        st = dict(misc=None, tok=None, feat=None, y=None, state=None, parts=[None, None], proj=None,
                  mom=None, recip=None, negp=None, maxp=None)
        exp_mark, st_mark, pv_mark, heads_evac = {}, {}, {}, {}
        headsT_read = {}
        rows_laid, mrows_laid = {}, {}
        v_ready, v_read = {}, {}
        main_end = {}

        def misc_job(emits):
            pe.wait(st["misc"])
            for f in emits[:-1]:
                pe.do(f)
            return pe.do(emits[-1], c_mi)

        def row_stats(src, ready, buf_free=None):
            dve.wait(ready, st["mom"])
            for t in range(NT):
                m = dve.do(lambda e, t=t: e.bn_stats(stats[:, t, :], src(t)), c_dve)
            dve.wait(m)
            for t in range(NT):
                m = dve.do(lambda e, t=t: e.bn_aggr(moments[:, t, :], stats[:, t, :]), c_dve)
            pool.wait(m)
            m = pool.do(lambda e: e.tensor_scalar(rstd[:, :], moments[:, :, 1], EPS, None, ALU.add), c_pool)
            pool.wait(m)
            return pool.do(lambda e: e.tensor_tensor(rstd[:, :], rstd[:, :], minus_half[:, :], ALU.pow), c_pool)

        def normalize(dst, src, ready, *free):
            pool.wait(ready, *free)
            for t in range(NT):
                m = pool.do(lambda e, t=t: e.tensor_scalar(dst(t), src(t), moments[:, t, 0:1], rstd[:, t:t + 1],
                                                           ALU.subtract, ALU.mult), c_pool)
            st["mom"] = m
            return m

        def project_qk(b):
            xb = x_sb[:, b % XS, :, :]
            if b + 1 < N and (b + 1) not in loaded:
                load_x(b + 1)
            ready = row_stats(lambda t: xb[:, t, :], loaded[b])
            yield
            ready = normalize(lambda t: tok[:, t, :], lambda t: xb[:, t, 0:D], ready, st["tok"])
            for _ in range(2):
                yield
            for h in range(NH):
                pe.wait(ready)
                m = misc_job([lambda e, t=t: e.transpose(misc_ps[:, t % TPH * P:(t % TPH + 1) * P], tok[:, t, :],
                                                         ident[:, :]) for t in range(h * TPH, (h + 1) * TPH)])
                st["tok"] = m
                act.wait(m, st["feat"])
                st["misc"] = feat_ready = act.do(lambda e, h=h: e.activation(
                    feat[:, h * BANK:(h + 1) * BANK], misc_ps[:, :], ACT.Copy), c_act)
                yield
            for i, w in enumerate((wq, wk)):
                for h in range(NH):
                    cols = slice(h * BANK, (h + 1) * BANK)
                    pe.wait(feat_ready)
                    m = misc_job([lambda e, w=w, c=cols: e.matmul(misc_ps[:, :], w[:, :], feat[:, c],
                                                                  start=True, stop=True)])
                    st["feat"] = m
                    act.wait(m, st["proj"], st["y"])
                    st["misc"] = got = act.do(lambda e: e.activation(proj_sb, misc_ps[:, :], ACT.Copy), c_act)
                    hi, mid, lo = (parts[:, i, j, cols] for j in range(3))
                    pool.wait(got, st["parts"][i])
                    m = pool.do(lambda e, hi=hi: e.tensor_copy(hi, proj_sb), c_pool)
                    pool.wait(m)
                    m = pool.do(lambda e, hi=hi: e.tensor_tensor(rest_sb, proj_sb, hi, ALU.subtract), c_pool)
                    st["proj"] = m
                    pool.wait(m)
                    m = pool.do(lambda e, mid=mid: e.tensor_copy(mid, rest_sb), c_pool)
                    pool.wait(m)
                    parts_ready = pool.do(lambda e, mid=mid, lo=lo: e.tensor_tensor(lo, rest_sb, mid, ALU.subtract),
                                          c_pool)
                    st["y"] = parts_ready
                    yield
            return feat_ready, parts_ready

        def lay_rows(b, parts_ready, *free):
            slot = b % 2
            sp.wait(parts_ready, *free)
            for i, rows in enumerate((q_rows, k_rows)):
                for side in range(2):
                    for n, term in enumerate(TERMS):
                        at = 64 * side + DH * n
                        m = sp.do(lambda e, i=i, s=side, at=at, part=term[i], rows=rows: e.dma_start(
                            rows[at:at + DH, slot, :, :], parts[64 * s:64 * s + 64, i, part, :]), c_rows[slot], 16)
            rows_laid[b] = m
            st["parts"] = [m, m]

        def project_v(b, feat_ready, *free):
            for h in range(NH):
                pe.wait(feat_ready)
                m = misc_job([lambda e, t=t: e.matmul(misc_ps[:, t % TPH * P:(t % TPH + 1) * P],
                                                      feat[:, t * P:(t + 1) * P], wv[:, :], start=True, stop=True)
                              for t in range(h * TPH, (h + 1) * TPH)])
                st["feat"] = m
                act.wait(m, *free)
                v_ready[b] = st["misc"] = act.do(lambda e, h=h: e.activation(
                    v_sb[:, b % 2, h * TPH:(h + 1) * TPH, :, 0:DH],
                    misc_ps[:, :].rearrange("p (t h d) -> p t h d", t=TPH, h=H), ACT.Copy), c_act)
                yield

        def divide_heads(b, h):
            for t in range(h * TPH, (h + 1) * TPH):
                cols = slice(t % TPH * P, (t % TPH + 1) * P)
                pe.wait(heads_evac[b, h])
                m = misc_job([lambda e, g=g, c=cols: e.transpose(misc_ps[:, g * P:(g + 1) * P], headsT[:, h, g, c],
                                                                 ident[:, :]) for g in range(NG)])
                headsT_read[b, h] = m
                by_head = misc_ps[:, :].rearrange("p (h c) -> p h c", h=H)
                dve.wait(m, st["recip"])
                m = dve.do(lambda e, v=by_head: e.reciprocal(recip[:, :], v[:, :, DH]), c_dve)
                dve.wait(m, st["tok"])
                st["misc"] = st["recip"] = done = dve.do(lambda e, t=t, v=by_head: e.tensor_tensor(
                    tok[:, t, :].rearrange("p (h d) -> p h d", h=H), v[:, :, 0:DH],
                    recip[:, :].unsqueeze(2).to_broadcast([P, H, DH]), ALU.mult), c_dve)
                divided[b, h] = done
                yield

        divided = {}

        def project_out(b):
            xb = x_sb[:, b % XS, :, :]
            for h in range(NH):
                pe.wait(divided[b, h])
                m = misc_job([lambda e, t=t: e.transpose(misc_ps[:, t % TPH * P:(t % TPH + 1) * P], tok[:, t, :],
                                                         ident[:, :]) for t in range(h * TPH, (h + 1) * TPH)])
                st["tok"] = m
                act.wait(m, st["feat"])
                st["misc"] = feat_ready = act.do(lambda e, h=h: e.activation(
                    feat[:, h * BANK:(h + 1) * BANK], misc_ps[:, :], ACT.Copy), c_act)
                yield
            for t in range(0, NT, 2):
                pe.wait(feat_ready)
                m = misc_job([lambda e, t=t, u=u: e.matmul(misc_ps[:, u * E:(u + 1) * E],
                                                           feat[:, (t + u) * P:(t + u + 1) * P], wo[:, :],
                                                           start=True, stop=True) for u in range(2)])
                st["feat"] = m
                dve.wait(m, st["y"])
                st["misc"] = y_ready = dve.do(lambda e, t=t: e.tensor_tensor(
                    y_sb[:, t:t + 2, :], misc_ps[:, :].rearrange("p (u e) -> p u e", u=2),
                    bo[:, :].unsqueeze(1).to_broadcast([P, 2, E]), ALU.add), c_dve)
                yield
            ready = row_stats(lambda t: y_sb[:, t, :], y_ready)
            yield
            ready = normalize(lambda t: y_sb[:, t, :], lambda t: y_sb[:, t, :], ready)
            pool.wait(ready)
            ready = pool.do(lambda e: e.tensor_tensor(xb, xb, y_sb[:, :, :], ALU.add), c_pool)
            for _ in range(4):
                yield
            ready = row_stats(lambda t: xb[:, t, :], ready)
            yield
            ready = normalize(lambda t: y_sb[:, t, :], lambda t: xb[:, t, :], ready)
            for _ in range(2):
                yield
            for half in range(2):
                for h in range(NH):
                    pe.wait(ready)
                    m = misc_job([lambda e, t=t, f=half: e.transpose(
                        misc_ps[:, t % TPH * P:(t % TPH + 1) * P], y_sb[:, t, f * P:(f + 1) * P], ident[:, :])
                        for t in range(h * TPH, (h + 1) * TPH)])
                    st["y"] = m
                    act.wait(m, st["state"], g_read.get(b - 1))
                    st["misc"] = state_ready[b] = act.do(lambda e, f=half, h=h: e.activation(
                        state[:, f, h * BANK:(h + 1) * BANK], misc_ps[:, :], ACT.Copy,
                        accum_out=sums[:, f, h:h + 1]), c_act)
                    yield

        state_ready, g_read, updated = {}, {}, {}

        def finish(b):
            slot = b % XS
            xb = x_sb[:, slot, :, :]
            for t in range(0, NT, 2):
                pe.wait(*updated[b])
                m = misc_job([lambda e, t=t, u=u, f=f: e.transpose(
                    misc_ps[:, u * E + f * P:u * E + (f + 1) * P], state[:, f, (t + u) * P:(t + u + 1) * P], ident[:, :])
                    for u in range(2) for f in range(2)])
                st["state"] = m
                act.wait(m, st["y"])
                st["misc"] = y_ready = act.do(lambda e, t=t: e.activation(
                    y_sb[:, t:t + 2, :], misc_ps[:, :].rearrange("p (u e) -> p u e", u=2), ACT.Copy), c_act)
                yield
            ready = row_stats(lambda t: y_sb[:, t, :], y_ready)
            yield
            ready = normalize(lambda t: y_sb[:, t, :], lambda t: y_sb[:, t, :], ready)
            pool.wait(ready)
            st["y"] = ready = pool.do(lambda e: e.tensor_tensor(xb, xb, y_sb[:, :, :], ALU.add), c_pool)
            sp.wait(ready)
            stored[b] = sp.do(lambda e: e.dma_start(out_dram[b], xb), c_out[slot], 16)
            yield

        def maxima(b):
            slot = b % 2
            n = 0
            for pair in range(HP):
                for side in range(2):
                    for qb in range(NT):
                        for kh in range(NH):
                            bank = max_ps[:, n % 2 * BANK:(n % 2 + 1) * BANK]
                            rows = slice(64 * side, 64 * side + ROWS)
                            pe.wait(rows_laid[b], reduced.get(n % 2))
                            m = pe.do(lambda e, bank=bank, r=rows, p=pair, q=qb, k=kh: e.matmul(
                                bank, q_rows[r, slot, p, q * P:(q + 1) * P], k_rows[r, slot, p, k * BANK:(k + 1) * BANK],
                                start=True, stop=True), c_mm)
                            dve.wait(m, st["maxp"])
                            col = (side * HP + pair) * NT + qb
                            reduced[n % 2] = dve.do(lambda e, bank=bank, k=kh, c=col: e.tensor_reduce(
                                max_parts[:, k, c:c + 1], bank, AX.X, ALU.max), c_red)
                            n += 1
                            yield
            max_ready[b] = reduced[(n - 1) % 2]

        reduced, max_ready = {}, {}

        def lay_maxima(b):
            slot = b % 2
            dve.wait(max_ready[b], st["maxall"] if "maxall" in st else None)
            st["maxp"] = m = dve.do(lambda e: e.tensor_tensor(max_all[:, :], max_parts[:, 0, :], max_parts[:, 1, :],
                                                              ALU.max), c_dve)
            pe.wait(m)
            st["maxall"] = m = misc_job([lambda e: e.transpose(misc_ps[:, 0:P], max_all[:, :], ident[:, :])])
            act.wait(m, st["neg"] if "neg" in st else None)
            st["misc"] = m = act.do(lambda e: e.activation(neg_max[:, :], misc_ps[:, 0:P], ACT.Copy, scale=-1.0),
                                    c_act)
            pool.wait(m, st["negp"])
            m = pool.do(lambda e: e.tensor_copy(neg_parts[:, 0, :], neg_max[:, :]), c_pool)
            pool.wait(m)
            m = pool.do(lambda e: e.tensor_tensor(neg_rest[:, :], neg_max[:, :], neg_parts[:, 0, :], ALU.subtract),
                        c_pool)
            st["neg"] = m
            pool.wait(m)
            m = pool.do(lambda e: e.tensor_copy(neg_parts[:, 1, :], neg_rest[:, :]), c_pool)
            pool.wait(m)
            m = pool.do(lambda e: e.tensor_tensor(neg_parts[:, 2, :], neg_rest[:, :], neg_parts[:, 1, :],
                                                  ALU.subtract), c_pool)
            sp.wait(m, main_end.get(b - 2))
            for side in range(2):
                for j in range(MROWS):
                    at = 64 * side + ROWS + j
                    m = sp.do(lambda e, s=side, j=j, at=at: e.dma_start(
                        q_rows[at:at + 1, slot, :, :], neg_parts[64 * s:64 * s + 64, j, :]), c_mrows[slot], 16)
            st["negp"] = mrows_laid[b] = m

        step_no = [0]

        def attention_steps(b):
            slot = b % 2
            todo = [(h, g, kb) for h in range(NH) for g in range(NG) for kb in range(NT)]
            last = None

            def scores(n, h, g, kb, two):
                pair = 2 * g + two
                pe.wait(rows_laid[b], mrows_laid[b], exp_mark.get((n - 1, two)), ffn_banks[0])
                for side in range(2):
                    rows = slice(64 * side, 64 * side + ROWS + MROWS)
                    bank = scoresT_ps[:, (2 * two + side) * BANK:(2 * two + side + 1) * BANK]
                    f = lambda e, r=rows, bank=bank: e.matmul(
                        bank, k_rows[r, slot, pair, kb * P:(kb + 1) * P], q_rows[r, slot, pair, h * BANK:(h + 1) * BANK],
                        start=True, stop=True)
                    m = pe.do(f, c_st if side else None)
                act.wait(m, pv_mark.get(n - NP), ffn_temps[0])
                exp_mark[n, two] = act.do(lambda e: e.activation(
                    p_sb[:, n % NP, 2 * two:2 * two + 2, :].rearrange("p h n -> p (h n)"),
                    scoresT_ps[:, 2 * two * BANK:(2 * two + 2) * BANK], ACT.Exp, scale=SCALE), c_exp)

            def weigh(n, h, g, kb):
                pe.wait(exp_mark[n, 0], exp_mark[n, 1], v_ready[b])
                if kb == 0:
                    pe.wait(heads_free[0])
                for j in range(4):
                    f = lambda e, j=j: e.matmul(
                        heads_ps[32 * j:32 * j + DH + 1, :], v_sb[:, slot, kb, 4 * g + j, 0:DH + 1],
                        p_sb[:, n % NP, j, :], start=(kb == 0), stop=(kb == NT - 1))
                    m = pe.do(f, c_pv if j == 3 else None)
                pv_mark[n] = m
                if kb == NT - 1:
                    dve.wait(m, headsT_read.get((b - 1, h)))
                    heads_free[0] = heads_evac[b, h] = dve.do(lambda e: e.tensor_copy(headsT[:, h, g, :], heads_ps[:, :]),
                                                              c_dve)

            for h, g, kb in todo:
                n = step_no[0]
                step_no[0] += 1
                scores(n, h, g, kb, 0)
                yield "piece"
                scores(n, h, g, kb, 1)
                yield "piece"
                if last:
                    weigh(*last)
                last = (n, h, g, kb)
                yield "step"
            weigh(*last)
            main_end[b] = pv_mark[last[0]]

        heads_free, ffn_banks, ffn_temps = [const_set], [None], [None]

        def coupling(b):
            h1 = lambda c, m: p_sb[:, 0, 2 * c + m, :]
            h2 = lambda c: p_sb[:, 1, c, :]
            h3 = lambda c: p_sb[0:D // 2, 1, 2 + c, :]
            tf = lambda c: p_sb[:, 2, c, :]
            twist_a, twist_b = p_sb[:, 2, 2, :], p_sb[:, 2, 3, :]
            bank = lambda c, i: scoresT_ps[:, (2 * c + i) * BANK:(2 * c + i + 1) * BANK]
            n = step_no[0] - 1
            before = [main_end.get(b + 1), exp_mark.get((n, 0)), exp_mark.get((n, 1))]
            pe.wait(*before)
            act.wait(*before)
            pool.wait(*before)
            dve.wait(*before)
            cols = [slice(c * BANK, (c + 1) * BANK) for c in range(NH)]
            ready = {c: [state_ready[b]] for c in range(NH)}
            wrote = {}
            tw = [None, None]
            gl = global_net(b)
            for cycle in range(3):
                last_mark = {}
                for c in range(NH):
                    pe.wait(*ready[c])
                    for m in range(2):
                        for k in range(2):
                            f = lambda e, c=c, m=m, k=k: e.matmul(bank(c, m), w1[:, k, m * P:(m + 1) * P],
                                                                  state[:, k, cols[c]], start=(k == 0), stop=(k == 1))
                            mk = pe.do(f, c_ff if k == 1 else None)
                        act.wait(mk)
                        wrote[c] = act.do(lambda e, c=c, m=m: e.activation(h1(c, m), bank(c, m), ACT.Gelu,
                                                                           bias=b1[:, m:m + 1]), c_act)
                        yield
                    if cycle == 0:
                        next(gl, None)
                for c in range(NH):
                    pe.wait(wrote[c])
                    for k in range(2):
                        mk = pe.do(lambda e, c=c, k=k: e.matmul(bank(c, 0), w2[:, k, :], h1(c, k), start=(k == 0),
                                                                stop=(k == 1)), c_ff if k == 1 else None)
                    act.wait(mk)
                    wrote[c] = act.do(lambda e, c=c: e.activation(h2(c), bank(c, 0), ACT.Gelu, bias=b2[:, 0:1]), c_act)
                    if cycle == 0:
                        next(gl, None)
                    yield
                for c in range(NH):
                    pe.wait(wrote[c])
                    mk = pe.do(lambda e, c=c: e.matmul(bank(c, 1)[0:D // 2, :], w3[:, :], h2(c), start=True, stop=True),
                               c_ff)
                    act.wait(mk)
                    wrote[c] = act.do(lambda e, c=c: e.activation(h3(c), bank(c, 1)[0:D // 2, :], ACT.Gelu,
                                                                  bias=b3[:, 0:1]), c_act)
                    yield
                for c in range(NH):
                    pe.wait(wrote[c])
                    mk = pe.do(lambda e, c=c: e.matmul(bank(c, 0), w4_all[:, :], h3(c), start=True, stop=True), c_ff)
                    ffn_banks_last[c] = mk
                    act.wait(mk, last_tf.get(c))
                    wrote[c] = act.do(lambda e, c=c: e.activation(tf(c), bank(c, 0), ACT.Tanh, bias=b4_half[:, 0:1],
                                                                  scale=0.5), c_act)
                    pool.wait(wrote[c], shift_ready[b])
                    cs = pool.do(lambda e, c=c: e.tensor_scalar(tf(c), tf(c), ar_token[:, 0:1], shift[:, 0:1],
                                                                ALU.mult, ALU.add), c_pool)
                    A, B = state[:, 0, cols[c]], state[:, 1, cols[c]]
                    pool.wait(cs, tw[0])
                    t1 = pool.do(lambda e, c=c, B=B: e.tensor_tensor(twist_a, tf(c), B, ALU.mult), c_pool)
                    dve.wait(cs, tw[1])
                    t2 = dve.do(lambda e, c=c, A=A: e.tensor_tensor(twist_b, tf(c), A, ALU.mult), c_dve)
                    pool.wait(t1, t2)
                    u1 = pool.do(lambda e, A=A: e.tensor_tensor(A, A, twist_a, ALU.add), c_pool)
                    dve.wait(t1, t2)
                    u2 = dve.do(lambda e, B=B: e.tensor_tensor(B, B, twist_b, ALU.subtract), c_dve)
                    tw = [u1, u2]
                    last_tf[c] = t2
                    ready[c] = [u1, u2]
                    yield
            updated[b] = [*ready[0], *ready[1]]
            ffn_banks[0] = wrote[NH - 1]
            ffn_temps[0] = tw[1]
            act.wait(tw[0])
            pe.wait(wrote[0], wrote[1])

        last_tf, ffn_banks_last, shift_ready = {}, {}, {}

        def global_net(b):
            dve.wait(state_ready[b])
            m = dve.do(lambda e: e.tensor_tensor(mean_g[:, :], sums[:, :, 0], sums[:, :, 1], ALU.add), c_dve)
            dve.wait(m)
            g_read[b] = m
            m = dve.do(lambda e: e.tensor_scalar(mean_g[:, :], mean_g[:, :], 1.0 / S, None, ALU.mult), c_dve)
            pe.wait(m)
            m = misc_job([lambda e, k=k: e.matmul(misc_ps[:, 0:1], g1[:, k, :], mean_g[:, k:k + 1], start=(k == 0),
                                                  stop=(k == 1)) for k in range(2)])
            act.wait(m)
            st["misc"] = m = act.do(lambda e: e.activation(hg1[:, :], misc_ps[:, 0:1], ACT.Gelu, bias=gb1[:, 0:1]), c_act)
            yield
            pe.wait(m)
            m = misc_job([lambda e: e.matmul(misc_ps[0:D // 2, 0:1], g2[:, :], hg1[:, :], start=True, stop=True)])
            act.wait(m)
            st["misc"] = m = act.do(lambda e: e.activation(hg2[:, :], misc_ps[0:D // 2, 0:1], ACT.Gelu,
                                                           bias=gb2[:, 0:1]), c_act)
            yield
            pe.wait(m)
            m = misc_job([lambda e: e.matmul(misc_ps[:, 0:1], g3_all[:, :], hg2[:, :], start=True, stop=True)])
            act.wait(m)
            st["misc"] = m = act.do(lambda e: e.activation(tg[:, :], misc_ps[:, 0:1], ACT.Tanh, bias=gb3_half[:, 0:1],
                                                           scale=0.5), c_act)
            pool.wait(m)
            shift_ready[b] = pool.do(lambda e: e.tensor_scalar(shift[:, :], tg[:, :], ar_global[:, 0:1], tenth[:, 0:1],
                                                               ALU.mult, ALU.add), c_pool)
            yield

        def valid(b):
            return 0 <= b < N

        def take(gen, n):
            for _ in range(n):
                if next(gen, "end") == "end":
                    return False
            return True

        def nothing():
            return
            yield

        MAX_PER_STEP = 3
        FFN_MAX = 4
        for b in range(-2, N + 2):
            kept = {}

            def background(b=b, kept=kept):
                if valid(b - 2):
                    yield from finish(b - 2)
                if valid(b - 1):
                    yield from divide_heads(b - 1, 1)
                    yield from project_out(b - 1)
                if valid(b + 2):
                    kept["qk"] = yield from project_qk(b + 2)

            back = background()
            mx = maxima(b + 1) if valid(b + 1) else nothing()
            if valid(b):
                steps = 0
                for what in attention_steps(b):
                    take(mx, 1)
                    if what == "step":
                        steps += 1
                        if not take(back, 1) and (b, 0) in heads_evac and steps > 36 and (b, 0) not in divided:
                            back = divide_heads(b, 0)
                            take(back, 1)
                take(back, 1000)
                if (b, 0) not in divided:
                    take(divide_heads(b, 0), 1000)
            else:
                while take(back, 1):
                    take(mx, 2)
            if valid(b + 2):
                lay_rows(b + 2, kept["qk"][1], main_end.get(b))
            if valid(b - 1):
                vp = project_v(b + 2, kept["qk"][0], main_end.get(b)) if valid(b + 2) else nothing()
                for n, _ in enumerate(coupling(b - 1)):
                    take(mx, FFN_MAX)
                    if n > 3:
                        take(vp, 1)
                    if valid(b + 1) and (b + 1) not in mrows_laid and not take(mx, 1):
                        lay_maxima(b + 1)
            elif valid(b + 2):
                take(project_v(b + 2, kept["qk"][0], main_end.get(b)), 1000)
            take(mx, 1000)
            if valid(b + 1) and (b + 1) not in mrows_laid:
                lay_maxima(b + 1)

        for b in range(max(0, N - XS), N):
            sp.wait(stored[b])

        block = ctx.enter_context(nc.Block())
        for register, queue in ((block.sync, sp), (block.tensor, pe), (block.scalar, act), (block.vector, dve),
                                (block.gpsimd, pool)):
            @register
            def _(e, queue=queue):
                for f in queue.items:
                    f(e)


def kernel(**inputs):
    import numpy as np
    import concourse.bacc as bacc
    from concourse.bass_utils import run_bass_kernel_spmd

    arr = {k: np.asarray(v) for k, v in inputs.items()}
    by_side = lambda w: np.ascontiguousarray(w.reshape(8, 2, 8, 128).transpose(3, 1, 2, 0).reshape(128, 128))
    given = {
        "x": arr["L0_attn_x"],
        "wq_t": by_side(arr["L0_attn_Wq"]), "wk_t": by_side(arr["L0_attn_Wk"]),
        "wv_t": np.ascontiguousarray(arr["L0_attn_Wv"].T), "wo_t": np.ascontiguousarray(arr["L0_attn_Wo"].T),
        "bo": arr["L0_attn_bo"],
        "w1": arr["L0_ffn_cn_w1"], "b1": arr["L0_ffn_cn_b1"], "w2": arr["L0_ffn_cn_w2"], "b2": arr["L0_ffn_cn_b2"],
        "w3": arr["L0_ffn_cn_w3"], "b3": arr["L0_ffn_cn_b3"], "w4": arr["L0_ffn_cn_w4"], "b4": arr["L0_ffn_cn_b4"],
        "g1": arr["L0_ffn_gc_w1"], "gb1": arr["L0_ffn_gc_b1"], "g2": arr["L0_ffn_gc_w2"], "gb2": arr["L0_ffn_gc_b2"],
        "g3": arr["L0_ffn_gc_w3"], "gb3": arr["L0_ffn_gc_b3"], "ar": arr["L0_ffn_adaptive_range"],
    }
    nc = bacc.Bacc("TRN2", target_bir_lowering=False, num_devices=1)
    arrays, aps = {}, {}
    for name, v in given.items():
        v = np.ascontiguousarray(v)
        arrays[f"in_{name}"] = v
        aps[name] = nc.dram_tensor(f"in_{name}", v.shape, mybir.dt.from_np(v.dtype), kind="ExternalInput").ap()
    aps["out"] = nc.dram_tensor("out", given["x"].shape, F32, kind="ExternalOutput").ap()
    attention_ffn_program(nc, aps)
    r = run_bass_kernel_spmd(nc, [arrays], core_ids=[0])
    return r.results[0]["out"]
```

```python
from contextlib import ExitStack

import concourse.bass as bass
from concourse import mybir

F32 = mybir.dt.float32
BF16 = mybir.dt.bfloat16
ACT = mybir.ActivationFunctionType
ALU = mybir.AluOpType
AX = mybir.AxisListType

P = 128
BANK = 512
EPS = 1e-5
TERMS = [(0, 0), (0, 1), (0, 2), (1, 0), (1, 1), (2, 0)]


class Queue:

    def __init__(self):
        self.items, self.seen, self.last = [], {}, None

    def wait(self, *marks):
        for mark in marks:
            if mark is None:
                continue
            sem, value = mark
            if self.seen.get(id(sem), 0) < value:
                self.seen[id(sem)] = value
                self.items.append(lambda e, s=sem.sem, v=value: e.wait_ge(s, v))

    def do(self, emit, sem=None, by=1):
        if sem is None:
            self.items.append(emit)
            return None
        sem.value += by
        self.items.append(lambda e: emit(e).then_inc(sem.sem, by))
        self.last = (sem, sem.value)
        return self.last


class Counter:

    def __init__(self, sem):
        self.sem, self.value = sem, 0


def attention_ffn_program(nc, a):
    N, S, E = a["x"].shape
    D = E // 2
    H = 16
    DH = D // H
    HP = H // 2
    NT = S // P
    NH = S // BANK
    TPH = BANK // P
    NG = H // 4
    ROWS = DH * len(TERMS)
    MROWS = 3
    SCALE = 1.0 / float(E // H) ** 0.5
    assert (S, E, DH, NH) == (1024, 256, 8, 2)

    x_dram = a["x"].rearrange("n (p t) e -> n p t e", p=P)
    out_dram = a["out"].rearrange("n (p t) e -> n p t e", p=P)

    with ExitStack() as ctx:
        def sb(name, shape, dt=F32):
            return ctx.enter_context(nc.sbuf_tensor(name, shape, dt))

        def counter(name):
            return Counter(ctx.enter_context(nc.semaphore(name)))

        scoresT_ps = ctx.enter_context(nc.psum_tensor("scoresT_ps", [P, 4 * BANK], F32))
        max_ps = ctx.enter_context(nc.psum_tensor("max_ps", [P, 2 * BANK], F32))
        heads_ps = ctx.enter_context(nc.psum_tensor("heads_ps", [P, BANK], F32))
        misc_ps = ctx.enter_context(nc.psum_tensor("misc_ps", [P, BANK], F32))

        XS = 2
        x_in = sb("x_in", [P, NT, E])
        x_sb = sb("x_sb", [P, XS, NT, E])
        q_rows = sb("q_rows", [P, 2, HP, S], BF16)
        k_rows = sb("k_rows", [P, 2, HP, S], BF16)
        q_pad = sb("q_pad", [P, 2, 2, 2, BANK], BF16)
        q_pad_max = sb("q_pad_max", [P, 2, S], BF16)
        v_sb = sb("v_sb", [P, 2, NT, H, DH + 2])
        NP = 2
        p_sb = sb("p_sb", [P, NP, 4, BANK])
        couple = sb("couple", [P, 4, BANK])
        headsT = sb("headsT", [P, NH, NG, BANK])
        parts = sb("parts", [P, 2, 3, S], BF16)
        tok = sb("tok", [P, NT, D])
        feat = sb("feat", [P, S])
        y_sb = sb("y_sb", [P, NT, E])
        y_flat = y_sb[:, :, :].rearrange("p t e -> p (t e)")
        proj_sb = [y_flat[:, 0:BANK], y_flat[:, BANK:2 * BANK]]
        rest_sb = [y_flat[:, 2 * BANK:3 * BANK], y_flat[:, 3 * BANK:4 * BANK]]
        state = sb("state", [P, 2, S])
        wq, wk, wv = sb("wq", [P, D]), sb("wk", [P, D]), sb("wv", [P, D])
        wo = sb("wo", [P, E])
        bo = sb("bo", [P, E])
        w1, w2, w3 = sb("w1", [P, 2, E]), sb("w2", [P, 2, D]), sb("w3", [P, D // 2])
        g1, g2 = sb("g1", [P, 2, D]), sb("g2", [P, D // 2])
        b1, b2, b3 = sb("b1", [P, 2]), sb("b2", [P, 1]), sb("b3", [D // 2, 1])
        gb1, gb2 = sb("gb1", [P, 1]), sb("gb2", [D // 2, 1])
        w4, g3 = sb("w4", [D // 2, 1]), sb("g3", [D // 2, 1])
        w4_all, g3_all = sb("w4_all", [D // 2, P]), sb("g3_all", [D // 2, P])
        b4, gb3, ar = sb("b4", [P, 1]), sb("gb3", [P, 1]), sb("ar", [P, 1])
        b4_half, gb3_half = sb("b4_half", [P, 1]), sb("gb3_half", [P, 1])
        ones = sb("ones", [D // 2, P])
        ident = sb("ident", [P, P])
        sign = sb("sign", [P, 1])
        tenth = sb("tenth", [P, 1])
        ar_token = sb("ar_token", [P, 1])
        ar_global = sb("ar_global", [P, 1])
        shift = sb("shift", [P, 1])
        max_parts = sb("max_parts", [P, 2, P])
        max_all = sb("max_all", [P, P])
        neg_max = sb("neg_max", [P, P])
        neg_rest = sb("neg_rest", [P, P])
        neg_parts = sb("neg_parts", [P, 3, P], BF16)
        stats = sb("stats", [P, NT, 6])
        moments = sb("moments", [P, NT, 2])
        rstd = sb("rstd", [P, NT])
        offset = sb("offset", [P, NT])
        minus_half = sb("minus_half", [P, NT])
        recip = sb("recip", [P, H])
        sums = sb("sums", [P, 2, NH])
        mean_g = sb("mean_g", [P, 2])
        hg1, hg2, tg = sb("hg1", [P, 1]), sb("hg2", [D // 2, 1]), sb("tg", [P, 1])

        c_w = counter("weights_loaded")
        c_xin = counter("x_in_loaded")
        c_x = [counter(f"x_loaded{i}") for i in range(XS)]
        c_out = [counter(f"out_stored{i}") for i in range(XS)]
        c_rows = [counter(f"rows_laid{i}") for i in range(2)]
        c_mrows = [counter(f"max_rows_laid{i}") for i in range(2)]
        c_set = counter("constants_set")
        c_set_p = counter("constants_pool")
        c_st = counter("scoresT_done")
        c_pv = counter("pv_done")
        c_mm = counter("max_scores_done")
        c_mi = counter("misc_mm_done")
        c_ff = counter("ffn_mm_done")
        c_exp = counter("exp_done")
        c_act = counter("act_misc_done")
        c_red = counter("max_taken")
        c_dve = counter("dve_misc_done")
        c_pool = counter("pool_done")
        c_pad = counter("q_padded")

        pe, act, dve, pool, sp = Queue(), Queue(), Queue(), Queue(), Queue()

        def load(dst, src):
            return sp.do(lambda e: e.dma_start(dst, src), c_w, 16)

        def load_x_in(b, free=None):
            sp.wait(free)
            loaded_in[b] = sp.do(lambda e: e.dma_start(x_in[:, :, :], x_dram[b]), c_xin, 16)

        def load_x(b):
            slot = b % XS
            if b >= XS:
                sp.wait(stored[b - XS])
            loaded[b] = sp.do(lambda e: e.dma_start(x_sb[:, slot, :, :], x_dram[b]), c_x[slot], 16)

        loaded_in, loaded, stored = {}, {}, {}
        load_x_in(0)
        load(wq[:, :], a["wq_t"])
        load(wk[:, :], a["wk_t"])
        load(wv[:, :], a["wv_t"])
        load(wo[:, :], a["wo_t"])
        load(bo[:, :], a["bo"].partition_broadcast(P))
        load(w1[:, :, :], a["w1"].rearrange("(k p) n -> p k n", p=P))
        load(w2[:, :, :], a["w2"].rearrange("(k p) n -> p k n", p=P))
        load(w3[:, :], a["w3"])
        load(w4[:, :], a["w4"])
        load(g1[:, :, :], a["g1"].rearrange("(k p) n -> p k n", p=P))
        load(g2[:, :], a["g2"])
        load(g3[:, :], a["g3"])
        for k in range(2):
            load(b1[:, k:k + 1], a["b1"][k * P:(k + 1) * P].rearrange("(p k) -> p k", k=1))
        load(b2[:, :], a["b2"].rearrange("(p k) -> p k", k=1))
        load(b3[:, :], a["b3"].rearrange("(p k) -> p k", k=1))
        load(gb1[:, :], a["gb1"].rearrange("(p k) -> p k", k=1))
        load(gb2[:, :], a["gb2"].rearrange("(p k) -> p k", k=1))
        load(b4[:, :], a["b4"].partition_broadcast(P))
        load(gb3[:, :], a["gb3"].partition_broadcast(P))
        weights = load(ar[:, :], a["ar"].partition_broadcast(P))

        m = pool.do(lambda e: e.memset(ident[:, :], 0.0), c_set_p)
        pool.wait(m)
        ident_set = pool.do(lambda e: e.affine_select(
            out=ident[:, :], in_=ident[:, :], compare_op=ALU.not_equal, fill=1.0, base=0,
            pattern=[[-1, P]], channel_multiplier=1), c_set_p)
        m = pool.do(lambda e: e.memset(minus_half[:, :], -0.5), c_set_p)
        m = pool.do(lambda e: e.memset(v_sb[:, :, :, :, DH:DH + 1], 1.0), c_set_p)
        for side in range(2):
            pool.wait(m)
            m = pool.do(lambda e, s=side: e.memset(k_rows[64 * s + 32:64 * s + 64, :, :, :], 1.0), c_set_p)
        rows_set = m
        pool.wait(rows_set)
        sp.wait(rows_set)
        pe.wait(ident_set, weights)

        def derive_constants():
            dve.do(lambda e: e.memset(heads_ps[:, :], 0.0))
            dve.do(lambda e: e.memset(sign[0:D // 2, :], 1.0))
            dve.do(lambda e: e.memset(sign[D // 2:D, :], -1.0))
            dve.do(lambda e: e.memset(q_pad[:, :, :, :, :], 0.0))
            dve.do(lambda e: e.memset(q_pad_max[:, :, :], 0.0))
            m = dve.do(lambda e: e.memset(ones[:, :], 1.0), c_set)
            dve.wait(m, weights)
            dve.do(lambda e: e.tensor_scalar(w4_all[:, :], ones[:, :], w4[:, 0:1], None, ALU.mult))
            dve.do(lambda e: e.tensor_scalar(g3_all[:, :], ones[:, :], g3[:, 0:1], None, ALU.mult))
            dve.do(lambda e: e.tensor_scalar(b4_half[:, :], b4[:, :], 0.5, None, ALU.mult))
            dve.do(lambda e: e.tensor_scalar(gb3_half[:, :], gb3[:, :], 0.5, None, ALU.mult))
            dve.do(lambda e: e.tensor_scalar(tenth[:, :], sign[:, :], 0.1, None, ALU.mult))
            dve.do(lambda e: e.tensor_scalar(ar_token[:, :], sign[:, :], ar[:, 0:1], 0.3, ALU.mult, ALU.mult))
            derived = dve.do(lambda e: e.tensor_scalar(ar_global[:, :], sign[:, :], ar[:, 0:1], 0.7,
                                                       ALU.mult, ALU.mult), c_set)
            heads_free[0] = derived
            pe.wait(derived, rows_set)
            act.wait(derived)
            pool.wait(derived)

        st = dict(misc=None, tok=None, feat=None, y=None, state=None, parts=[None, None], proj=[None, None], rest=[None, None],
                  mom=None, recip=None, negp=None, maxp=None)
        exp_mark, st_mark, pv_mark, heads_evac = {}, {}, {}, {}
        headsT_read = {}
        rows_laid, mrows_laid = {}, {}
        v_ready, v_read = {}, {}
        main_end = {}

        def pause(n):
            for _ in range(n):
                yield

        def misc_job(emits):
            pe.wait(st["misc"])
            for f in emits[:-1]:
                pe.do(f)
            return pe.do(emits[-1], c_mi)

        def row_stats(src, ready, buf_free=None):
            dve.wait(ready, st["mom"])
            for t in range(NT):
                m = dve.do(lambda e, t=t: e.bn_stats(stats[:, t, :], src(t)), c_dve)
                yield
            dve.wait(m)
            for t in range(NT):
                m = dve.do(lambda e, t=t: e.bn_aggr(moments[:, t, :], stats[:, t, :]), c_dve)
            pool.wait(m)
            m = pool.do(lambda e: e.tensor_scalar(rstd[:, :], moments[:, :, 1], EPS, None, ALU.add), c_pool)
            pool.wait(m)
            m = pool.do(lambda e: e.tensor_tensor(rstd[:, :], rstd[:, :], minus_half[:, :], ALU.pow), c_pool)
            m = pool.do(lambda e: e.tensor_scalar(offset[:, :], moments[:, :, 0], -1.0, None, ALU.mult), c_pool)
            pool.wait(m)
            return pool.do(lambda e: e.tensor_tensor(offset[:, :], offset[:, :], rstd[:, :], ALU.mult), c_pool)

        def normalize(dst, src, ready, *free):
            act.wait(ready, *free)
            for t in range(NT):
                m = act.do(lambda e, t=t: e.activation(dst(t), src(t), ACT.Identity, bias=offset[:, t:t + 1],
                                                       scale=rstd[:, t:t + 1]), c_act)
                yield
            st["mom"] = m
            return m

        def project_qk(b):
            ready = yield from row_stats(lambda t: x_in[:, t, :], loaded_in[b])
            yield from pause(3)
            ready = yield from normalize(lambda t: tok[:, t, :], lambda t: x_in[:, t, 0:D], ready, st["tok"])
            if b + 1 < N:
                load_x_in(b + 1, ready)
            for h in range(NH):
                pe.wait(ready)
                m = misc_job([lambda e, t=t: e.transpose(misc_ps[:, t % TPH * P:(t % TPH + 1) * P], tok[:, t, :],
                                                         ident[:, :]) for t in range(h * TPH, (h + 1) * TPH)])
                st["tok"] = m
                act.wait(m, st["feat"])
                st["misc"] = feat_ready = act.do(lambda e, h=h: e.activation(
                    feat[:, h * BANK:(h + 1) * BANK], misc_ps[:, :], ACT.Copy), c_act)
                yield from pause(2)
            for i, w in enumerate((wq, wk)):
                for h in range(NH):
                    cols = slice(h * BANK, (h + 1) * BANK)
                    pe.wait(feat_ready)
                    m = misc_job([lambda e, w=w, c=cols: e.matmul(misc_ps[:, :], w[:, :], feat[:, c],
                                                                  start=True, stop=True)])
                    st["feat"] = m
                    hi, mid, lo = (parts[:, i, j, cols] for j in range(3))
                    proj, rest = proj_sb[h], rest_sb[h]
                    act.wait(m, st["proj"][h], st["y"], st["parts"][i])
                    got = act.do(lambda e, proj=proj: e.activation(proj, misc_ps[:, :], ACT.Copy), c_act)
                    st["misc"] = got = act.do(lambda e, hi=hi: e.activation(hi, misc_ps[:, :], ACT.Copy), c_act)
                    pool.wait(got, st["rest"][h])
                    m = pool.do(lambda e, hi=hi, proj=proj, rest=rest: e.tensor_tensor(rest, proj, hi, ALU.subtract),
                                c_pool)
                    st["proj"][h] = m
                    yield from pause(3)
                    dve.wait(m)
                    m = dve.do(lambda e, mid=mid, rest=rest: e.tensor_copy(mid, rest), c_dve)
                    pool.wait(m)
                    st["rest"][h] = parts_ready = pool.do(
                        lambda e, mid=mid, lo=lo, rest=rest: e.tensor_tensor(lo, rest, mid, ALU.subtract), c_pool)
                    yield
            st["y"] = parts_ready
            return feat_ready, parts_ready

        def lay_rows(b, parts_ready, *free):
            slot = b % 2
            sp.wait(parts_ready, *free)
            for i, rows in enumerate((q_rows, k_rows)):
                for side in range(2):
                    for n, term in enumerate(TERMS):
                        at = 64 * side + DH * n
                        m = sp.do(lambda e, i=i, s=side, at=at, part=term[i], rows=rows: e.dma_start(
                            rows[at:at + DH, slot, :, :], parts[64 * s:64 * s + 64, i, part, :]), c_rows[slot], 16)
            rows_laid[b] = m
            st["parts"] = [m, m]

        def project_v(b, feat_ready, *free):
            for h in range(NH):
                pe.wait(feat_ready)
                m = misc_job([lambda e, t=t: e.matmul(misc_ps[:, t % TPH * P:(t % TPH + 1) * P],
                                                      feat[:, t * P:(t + 1) * P], wv[:, :], start=True, stop=True)
                              for t in range(h * TPH, (h + 1) * TPH)])
                st["feat"] = m
                act.wait(m, *free)
                v_ready[b] = st["misc"] = act.do(lambda e, h=h: e.activation(
                    v_sb[:, b % 2, h * TPH:(h + 1) * TPH, :, 0:DH],
                    misc_ps[:, :].rearrange("p (t h d) -> p t h d", t=TPH, h=H), ACT.Copy), c_act)
                yield

        def divide_heads(b, h):
            for t in range(h * TPH, (h + 1) * TPH):
                cols = slice(t % TPH * P, (t % TPH + 1) * P)
                pe.wait(heads_evac[b, h])
                m = misc_job([lambda e, g=g, c=cols: e.transpose(misc_ps[:, g * P:(g + 1) * P], headsT[:, h, g, c],
                                                                 ident[:, :]) for g in range(NG)])
                headsT_read[b, h] = m
                by_head = misc_ps[:, :].rearrange("p (h c) -> p h c", h=H)
                dve.wait(m, st["recip"])
                m = dve.do(lambda e, v=by_head: e.reciprocal(recip[:, :], v[:, :, DH]), c_dve)
                dve.wait(m, st["tok"])
                st["misc"] = st["recip"] = done = dve.do(lambda e, t=t, v=by_head: e.tensor_tensor(
                    tok[:, t, :].rearrange("p (h d) -> p h d", h=H), v[:, :, 0:DH],
                    recip[:, :].unsqueeze(2).to_broadcast([P, H, DH]), ALU.mult), c_dve)
                divided[b, h] = done
                yield from pause(2)

        divided = {}

        def project_out(b):
            xb = x_sb[:, b % XS, :, :]
            for h in range(NH):
                pe.wait(divided[b, h])
                m = misc_job([lambda e, t=t: e.transpose(misc_ps[:, t % TPH * P:(t % TPH + 1) * P], tok[:, t, :],
                                                         ident[:, :]) for t in range(h * TPH, (h + 1) * TPH)])
                st["tok"] = m
                act.wait(m, st["feat"])
                st["misc"] = feat_ready = act.do(lambda e, h=h: e.activation(
                    feat[:, h * BANK:(h + 1) * BANK], misc_ps[:, :], ACT.Copy), c_act)
                yield from pause(2)
            for t in range(0, NT, 2):
                pe.wait(feat_ready)
                m = misc_job([lambda e, t=t, u=u: e.matmul(misc_ps[:, u * E:(u + 1) * E],
                                                           feat[:, (t + u) * P:(t + u + 1) * P], wo[:, :],
                                                           start=True, stop=True) for u in range(2)])
                st["feat"] = m
                dve.wait(m, st["y"])
                st["misc"] = y_ready = dve.do(lambda e, t=t: e.tensor_tensor(
                    y_sb[:, t:t + 2, :], misc_ps[:, :].rearrange("p (u e) -> p u e", u=2),
                    bo[:, :].unsqueeze(1).to_broadcast([P, 2, E]), ALU.add), c_dve)
                yield from pause(2)
            ready = yield from row_stats(lambda t: y_sb[:, t, :], y_ready)
            yield from pause(3)
            ready = yield from normalize(lambda t: y_sb[:, t, :], lambda t: y_sb[:, t, :], ready)
            pool.wait(ready, loaded[b])
            ready = pool.do(lambda e: e.tensor_tensor(xb, xb, y_sb[:, :, :], ALU.add), c_pool)
            yield from pause(8)
            ready = yield from row_stats(lambda t: xb[:, t, :], ready)
            yield from pause(3)
            ready = yield from normalize(lambda t: y_sb[:, t, :], lambda t: xb[:, t, :], ready)
            for half in range(2):
                for h in range(NH):
                    pe.wait(ready)
                    m = misc_job([lambda e, t=t, f=half: e.transpose(
                        misc_ps[:, t % TPH * P:(t % TPH + 1) * P], y_sb[:, t, f * P:(f + 1) * P], ident[:, :])
                        for t in range(h * TPH, (h + 1) * TPH)])
                    st["y"] = m
                    act.wait(m, st["state"], g_read.get(b - 1))
                    st["misc"] = state_ready[b] = act.do(lambda e, f=half, h=h: e.activation(
                        state[:, f, h * BANK:(h + 1) * BANK], misc_ps[:, :], ACT.Copy,
                        accum_out=sums[:, f, h:h + 1]), c_act)
                    yield from pause(2)

        state_ready, g_read, updated = {}, {}, {}

        def finish(b):
            slot = b % XS
            xb = x_sb[:, slot, :, :]
            for t in range(0, NT, 2):
                pe.wait(*updated[b])
                m = misc_job([lambda e, t=t, u=u, f=f: e.transpose(
                    misc_ps[:, u * E + f * P:u * E + (f + 1) * P], state[:, f, (t + u) * P:(t + u + 1) * P], ident[:, :])
                    for u in range(2) for f in range(2)])
                st["state"] = m
                act.wait(m, st["y"])
                st["misc"] = y_ready = act.do(lambda e, t=t: e.activation(
                    y_sb[:, t:t + 2, :], misc_ps[:, :].rearrange("p (u e) -> p u e", u=2), ACT.Copy), c_act)
                yield from pause(2)
            ready = yield from row_stats(lambda t: y_sb[:, t, :], y_ready)
            yield from pause(3)
            ready = yield from normalize(lambda t: y_sb[:, t, :], lambda t: y_sb[:, t, :], ready)
            pool.wait(ready)
            st["y"] = ready = pool.do(lambda e: e.tensor_tensor(xb, xb, y_sb[:, :, :], ALU.add), c_pool)
            sp.wait(ready)
            stored[b] = sp.do(lambda e: e.dma_start(out_dram[b], xb), c_out[slot], 16)
            yield

        def maxima(b):
            slot = b % 2
            n = 0
            dve.wait(rows_laid[b])

            def pad(pair, side):
                rows = slice(64 * side, 64 * side + ROWS)
                dve.wait(pad_read.get(side))
                return dve.do(lambda e: e.tensor_copy(q_pad_max[rows, side, :], q_rows[rows, slot, pair, :]), c_pad)

            padded = {(0, 0): pad(0, 0)}
            for pair in range(HP):
                for side in range(2):
                    ahead = (pair, 1) if side == 0 else (pair + 1, 0)
                    if ahead[0] < HP:
                        padded[ahead] = pad(*ahead)
                    for qb in range(NT):
                        for kh in range(NH):
                            bank = max_ps[:, n % 2 * BANK:(n % 2 + 1) * BANK]
                            pe.wait(padded[pair, side], reduced.get(n % 2))
                            pad_read[side] = m = pe.do(lambda e, bank=bank, s=side, p=pair, q=qb, k=kh: e.matmul(
                                bank, q_pad_max[:, s, q * P:(q + 1) * P], k_rows[:, slot, p, k * BANK:(k + 1) * BANK],
                                start=True, stop=True), c_mm)
                            dve.wait(m, st["maxp"])
                            col = (side * HP + pair) * NT + qb
                            reduced[n % 2] = dve.do(lambda e, bank=bank, k=kh, c=col: e.tensor_reduce(
                                max_parts[:, k, c:c + 1], bank, AX.X, ALU.max), c_red)
                            n += 1
                            yield
            max_ready[b] = reduced[(n - 1) % 2]

        stream = dict(batch=0, units=None, laying=None)

        def take_maxima(n):
            for _ in range(n):
                b = stream["batch"]
                if stream["units"] is None and b < N and b in rows_laid:
                    stream["units"] = maxima(b)
                if stream["units"] is not None and next(stream["units"], "end") == "end":
                    stream["laying"] = lay_maxima(b)
                    next(stream["laying"])
                    stream["units"] = None
                    stream["batch"] += 1
                elif stream["laying"] is not None and next(stream["laying"], "end") == "end":
                    stream["laying"] = None

        reduced, max_ready, pad_read = {}, {}, {}

        def lay_maxima(b):
            slot = b % 2
            dve.wait(max_ready[b], st["maxall"] if "maxall" in st else None)
            st["maxp"] = m = dve.do(lambda e: e.tensor_tensor(max_all[:, :], max_parts[:, 0, :], max_parts[:, 1, :],
                                                              ALU.max), c_dve)
            yield
            yield
            pe.wait(m)
            st["maxall"] = m = misc_job([lambda e: e.transpose(misc_ps[:, 0:P], max_all[:, :], ident[:, :])])
            act.wait(m, st["neg"] if "neg" in st else None)
            st["misc"] = m = act.do(lambda e: e.activation(neg_max[:, :], misc_ps[:, 0:P], ACT.Copy, scale=-1.0),
                                    c_act)
            pool.wait(m, st["negp"])
            m = pool.do(lambda e: e.tensor_copy(neg_parts[:, 0, :], neg_max[:, :]), c_pool)
            pool.wait(m)
            m = pool.do(lambda e: e.tensor_tensor(neg_rest[:, :], neg_max[:, :], neg_parts[:, 0, :], ALU.subtract),
                        c_pool)
            st["neg"] = m
            pool.wait(m)
            m = pool.do(lambda e: e.tensor_copy(neg_parts[:, 1, :], neg_rest[:, :]), c_pool)
            pool.wait(m)
            m = pool.do(lambda e: e.tensor_tensor(neg_parts[:, 2, :], neg_rest[:, :], neg_parts[:, 1, :],
                                                  ALU.subtract), c_pool)
            sp.wait(m, main_end.get(b - 2))
            for side in range(2):
                for j in range(MROWS):
                    at = 64 * side + ROWS + j
                    m = sp.do(lambda e, s=side, j=j, at=at: e.dma_start(
                        q_rows[at:at + 1, slot, :, :], neg_parts[64 * s:64 * s + 64, j, :]), c_mrows[slot], 16)
            st["negp"] = mrows_laid[b] = m
            for _ in range(12):
                yield
            pad_unit(b, 0, 0)

        step_no = [0]

        def pad_unit(b, h, g):
            u = (h * NG + g) % 2
            dve.wait(rows_laid[b], mrows_laid[b], unit_read.get((0, u)))
            for side in range(2):
                rows = slice(64 * side, 64 * side + ROWS + MROWS)
                padded[b, h, g] = dve.do(lambda e, r=rows, s=side: e.tensor_copy(
                    q_pad[r, u, s, :, :], q_rows[r, b % 2, 2 * g:2 * g + 2, h * BANK:(h + 1) * BANK]), c_pad)

        padded = {}

        def attention_steps(b):
            slot = b % 2
            todo = [(h, g, kb) for h in range(NH) for g in range(NG) for kb in range(NT)]
            last = None

            def scores(n, h, g, kb, two):
                pair = 2 * g + two
                pe.wait(padded[b, h, g], exp_mark.get((n - 1, two)), ffn_banks[0])
                for side in range(2):
                    bank = scoresT_ps[:, (2 * two + side) * BANK:(2 * two + side + 1) * BANK]
                    f = lambda e, s=side, bank=bank: e.matmul(
                        bank, k_rows[:, slot, pair, kb * P:(kb + 1) * P], q_pad[:, (h * NG + g) % 2, s, two, :],
                        start=True, stop=True)
                    m = pe.do(f, c_st if side else None)
                unit_read[0, (h * NG + g) % 2] = m
                act.wait(m, pv_mark.get(n - NP), ffn_temps[0])
                exp_mark[n, two] = act.do(lambda e: e.activation(
                    p_sb[:, n % NP, 2 * two:2 * two + 2, :].rearrange("p h n -> p (h n)"),
                    scoresT_ps[:, 2 * two * BANK:(2 * two + 2) * BANK], ACT.Exp, scale=SCALE), c_exp)

            def weigh(n, h, g, kb):
                pe.wait(exp_mark[n, 0], exp_mark[n, 1], v_ready[b])
                if kb == 0:
                    pe.wait(heads_free[0])
                for j in range(4):
                    f = lambda e, j=j: e.matmul(
                        heads_ps[32 * j:32 * j + DH + 1, :], v_sb[:, slot, kb, 4 * g + j, 0:DH + 1],
                        p_sb[:, n % NP, j, :], start=(kb == 0), stop=(kb == NT - 1))
                    m = pe.do(f, c_pv if j == 3 else None)
                pv_mark[n] = m
                if kb == NT - 1:
                    act.wait(m, headsT_read.get((b - 1, h)))
                    heads_free[0] = heads_evac[b, h] = act.do(lambda e: e.activation(
                        headsT[:, h, g, :], heads_ps[:, :], ACT.Copy), c_act)

            units = [(h, g) for h in range(NH) for g in range(NG)]
            if (b, 0, 0) not in padded:
                pad_unit(b, 0, 0)
            for h, g, kb in todo:
                nxt = units.index((h, g)) + 1
                if kb == 0 and nxt < len(units):
                    pad_unit(b, *units[nxt])
                n = step_no[0]
                step_no[0] += 1
                scores(n, h, g, kb, 0)
                yield "piece"
                scores(n, h, g, kb, 1)
                yield "piece"
                if last:
                    weigh(*last)
                last = (n, h, g, kb)
                yield "step"
            weigh(*last)
            main_end[b] = pv_mark[last[0]]

        unit_read = {}
        heads_free, ffn_banks, ffn_temps = [None], [None], [None]

        def coupling(b):
            h1 = lambda c, m: p_sb[:, 0, 2 * c + m, :]
            h2 = lambda c: p_sb[:, 1, c, :]
            h3 = lambda c: p_sb[0:D // 2, 1, 2 + c, :]
            tf = lambda c: couple[:, c, :]
            twist_a, twist_b = couple[:, 2, :], couple[:, 3, :]
            bank = lambda c, i: scoresT_ps[:, (2 * c + i) * BANK:(2 * c + i + 1) * BANK]
            n = step_no[0] - 1
            before = [main_end.get(b + 1), exp_mark.get((n, 0)), exp_mark.get((n, 1))]
            pe.wait(*before)
            act.wait(*before)
            pool.wait(*before)
            dve.wait(*before)
            cols = [slice(c * BANK, (c + 1) * BANK) for c in range(NH)]
            ready = {c: [state_ready[b]] for c in range(NH)}
            tw = [None, None]
            gl = global_net(b)
            for cycle in range(3):
                for c in range(NH):
                    pe.wait(*ready[c])
                    for m in range(2):
                        for k in range(2):
                            mk = pe.do(lambda e, c=c, m=m, k=k: e.matmul(
                                bank(c, m), w1[:, k, m * P:(m + 1) * P], state[:, k, cols[c]], start=(k == 0),
                                stop=(k == 1)), c_ff if k == 1 else None)
                        act.wait(mk)
                        wrote = act.do(lambda e, c=c, m=m: e.activation(h1(c, m), bank(c, m), ACT.Gelu,
                                                                        bias=b1[:, m:m + 1]), c_act)
                        yield "short" if m == 0 else "long"
                    next(gl, None)
                    pe.wait(wrote)
                    for k in range(2):
                        mk = pe.do(lambda e, c=c, k=k: e.matmul(bank(c, 0), w2[:, k, :], h1(c, k), start=(k == 0),
                                                                stop=(k == 1)), c_ff if k == 1 else None)
                    act.wait(mk)
                    wrote = act.do(lambda e, c=c: e.activation(h2(c), bank(c, 0), ACT.Gelu, bias=b2[:, 0:1]), c_act)
                    yield "long"
                    next(gl, None)
                    pe.wait(wrote)
                    mk = pe.do(lambda e, c=c: e.matmul(bank(c, 1)[0:D // 2, :], w3[:, :], h2(c), start=True, stop=True),
                               c_ff)
                    act.wait(mk)
                    wrote = act.do(lambda e, c=c: e.activation(h3(c), bank(c, 1)[0:D // 2, :], ACT.Gelu,
                                                               bias=b3[:, 0:1]), c_act)
                    yield "long"
                    next(gl, None)
                    pe.wait(wrote)
                    mk = pe.do(lambda e, c=c: e.matmul(bank(c, 0), w4_all[:, :], h3(c), start=True, stop=True), c_ff)
                    act.wait(mk, *(last_tf.get(c) or ()))
                    wrote = act.do(lambda e, c=c: e.activation(tf(c), bank(c, 0), ACT.Tanh, bias=b4_half[:, 0:1],
                                                               scale=0.5), c_act)
                    pool.wait(wrote, shift_ready[b])
                    cs = pool.do(lambda e, c=c: e.tensor_scalar(tf(c), tf(c), ar_token[:, 0:1], shift[:, 0:1],
                                                                ALU.mult, ALU.add), c_pool)
                    A, B = state[:, 0, cols[c]], state[:, 1, cols[c]]
                    pool.wait(cs, tw[0])
                    t1 = pool.do(lambda e, c=c, B=B: e.tensor_tensor(twist_a, tf(c), B, ALU.mult), c_pool)
                    dve.wait(cs, tw[1])
                    t2 = dve.do(lambda e, c=c, A=A: e.tensor_tensor(twist_b, tf(c), A, ALU.mult), c_dve)
                    yield "none"
                    pool.wait(t1, t2)
                    u1 = pool.do(lambda e, A=A: e.tensor_tensor(A, A, twist_a, ALU.add), c_pool)
                    dve.wait(t1, t2)
                    u2 = dve.do(lambda e, B=B: e.tensor_tensor(B, B, twist_b, ALU.subtract), c_dve)
                    tw = [u1, u2]
                    last_tf[c] = [t1, t2]
                    ready[c] = [u1, u2]
            updated[b] = [*ready[0], *ready[1]]
            ffn_banks[0] = wrote
            ffn_temps[0] = mk

        last_tf, shift_ready = {}, {}

        def global_net(b):
            dve.wait(state_ready[b])
            m = dve.do(lambda e: e.tensor_tensor(mean_g[:, :], sums[:, :, 0], sums[:, :, 1], ALU.add), c_dve)
            dve.wait(m)
            g_read[b] = m
            m = dve.do(lambda e: e.tensor_scalar(mean_g[:, :], mean_g[:, :], 1.0 / S, None, ALU.mult), c_dve)
            pe.wait(m)
            m = misc_job([lambda e, k=k: e.matmul(misc_ps[:, 0:1], g1[:, k, :], mean_g[:, k:k + 1], start=(k == 0),
                                                  stop=(k == 1)) for k in range(2)])
            act.wait(m)
            st["misc"] = m = act.do(lambda e: e.activation(hg1[:, :], misc_ps[:, 0:1], ACT.Gelu, bias=gb1[:, 0:1]), c_act)
            yield
            pe.wait(m)
            m = misc_job([lambda e: e.matmul(misc_ps[0:D // 2, 0:1], g2[:, :], hg1[:, :], start=True, stop=True)])
            act.wait(m)
            st["misc"] = m = act.do(lambda e: e.activation(hg2[:, :], misc_ps[0:D // 2, 0:1], ACT.Gelu,
                                                           bias=gb2[:, 0:1]), c_act)
            yield
            pe.wait(m)
            m = misc_job([lambda e: e.matmul(misc_ps[:, 0:1], g3_all[:, :], hg2[:, :], start=True, stop=True)])
            act.wait(m)
            st["misc"] = m = act.do(lambda e: e.activation(tg[:, :], misc_ps[:, 0:1], ACT.Tanh, bias=gb3_half[:, 0:1],
                                                           scale=0.5), c_act)
            pool.wait(m)
            shift_ready[b] = pool.do(lambda e: e.tensor_scalar(shift[:, :], tg[:, :], ar_global[:, 0:1], tenth[:, 0:1],
                                                               ALU.mult, ALU.add), c_pool)
            yield

        def valid(b):
            return 0 <= b < N

        def take(gen, n):
            for _ in range(n):
                if next(gen, "end") == "end":
                    return False
            return True

        def nothing():
            return
            yield

        for b in range(-2, N + 2):
            kept = {}
            if valid(b - 1) and (b - 1) not in loaded:
                load_x(b - 1)

            def background(b=b, kept=kept):
                if valid(b - 2):
                    yield from finish(b - 2)
                if valid(b - 1):
                    yield from divide_heads(b - 1, 1)
                    yield from project_out(b - 1)
                if valid(b + 2):
                    kept["qk"] = yield from project_qk(b + 2)

            back = background()
            if valid(b):
                while (b, 0, 0) not in padded:
                    take_maxima(1)
                pieces, first_half = 0, 3 * (NG * NT + 2)
                for _ in attention_steps(b):
                    pieces += 1
                    take_maxima(1 + (pieces % 12 == 0))
                    if not take(back, 1) and pieces > first_half and (b, 0) not in divided:
                        back = divide_heads(b, 0)
                        take(back, 1)
                take(back, 1000)
                if (b, 0) not in divided:
                    take(divide_heads(b, 0), 1000)
            else:
                while take(back, 1):
                    take_maxima(2)
                if b == -2:
                    derive_constants()
            values = nothing()
            if valid(b + 2):
                lay_rows(b + 2, kept["qk"][1], main_end.get(b))
                values = project_v(b + 2, kept["qk"][0], main_end.get(b))
            if valid(b - 1):
                for n, gap in enumerate(coupling(b - 1)):
                    take_maxima({"none": 0, "short": 2, "long": 2}[gap])
                    if n % 4 == 3:
                        take(values, 1)
            take(values, 1000)

        for b in range(max(0, N - XS), N):
            sp.wait(stored[b])

        block = ctx.enter_context(nc.Block())
        for register, queue in ((block.sync, sp), (block.tensor, pe), (block.scalar, act), (block.vector, dve),
                                (block.gpsimd, pool)):
            @register
            def _(e, queue=queue):
                for f in queue.items:
                    f(e)


def kernel(**inputs):
    import numpy as np
    import concourse.bacc as bacc
    from concourse.bass_utils import run_bass_kernel_spmd

    arr = {k: np.asarray(v) for k, v in inputs.items()}
    by_side = lambda w: np.ascontiguousarray(w.reshape(8, 2, 8, 128).transpose(3, 1, 2, 0).reshape(128, 128))
    given = {
        "x": arr["L0_attn_x"],
        "wq_t": by_side(arr["L0_attn_Wq"]), "wk_t": by_side(arr["L0_attn_Wk"]),
        "wv_t": np.ascontiguousarray(arr["L0_attn_Wv"].T), "wo_t": np.ascontiguousarray(arr["L0_attn_Wo"].T),
        "bo": arr["L0_attn_bo"],
        "w1": arr["L0_ffn_cn_w1"], "b1": arr["L0_ffn_cn_b1"], "w2": arr["L0_ffn_cn_w2"], "b2": arr["L0_ffn_cn_b2"],
        "w3": arr["L0_ffn_cn_w3"], "b3": arr["L0_ffn_cn_b3"], "w4": arr["L0_ffn_cn_w4"], "b4": arr["L0_ffn_cn_b4"],
        "g1": arr["L0_ffn_gc_w1"], "gb1": arr["L0_ffn_gc_b1"], "g2": arr["L0_ffn_gc_w2"], "gb2": arr["L0_ffn_gc_b2"],
        "g3": arr["L0_ffn_gc_w3"], "gb3": arr["L0_ffn_gc_b3"], "ar": arr["L0_ffn_adaptive_range"],
    }
    nc = bacc.Bacc("TRN2", target_bir_lowering=False, num_devices=1)
    arrays, aps = {}, {}
    for name, v in given.items():
        v = np.ascontiguousarray(v)
        arrays[f"in_{name}"] = v
        aps[name] = nc.dram_tensor(f"in_{name}", v.shape, mybir.dt.from_np(v.dtype), kind="ExternalInput").ap()
    aps["out"] = nc.dram_tensor("out", given["x"].shape, F32, kind="ExternalOutput").ap()
    attention_ffn_program(nc, aps)
    r = run_bass_kernel_spmd(nc, [arrays], core_ids=[0])
    return r.results[0]["out"]
```

```python
from contextlib import ExitStack

import concourse.bass as bass
from concourse import mybir

F32 = mybir.dt.float32
BF16 = mybir.dt.bfloat16
ACT = mybir.ActivationFunctionType
ALU = mybir.AluOpType
AX = mybir.AxisListType

P = 128
BANK = 512
EPS = 1e-5
TWO_ONES = 1.0 + 16256 * 2.0 ** -23
TERMS = [(0, 0), (0, 1), (0, 2), (1, 0), (1, 1), (2, 0)]


class Queue:

    def __init__(self):
        self.items, self.seen, self.last = [], {}, None

    def wait(self, *marks):
        for mark in marks:
            if mark is None:
                continue
            sem, value = mark
            if self.seen.get(id(sem), 0) < value:
                self.seen[id(sem)] = value
                self.items.append(lambda e, s=sem.sem, v=value: e.wait_ge(s, v))

    def do(self, emit, sem=None, by=1):
        if sem is None:
            self.items.append(emit)
            return None
        sem.value += by
        self.items.append(lambda e: emit(e).then_inc(sem.sem, by))
        self.last = (sem, sem.value)
        return self.last


class Counter:

    def __init__(self, sem):
        self.sem, self.value = sem, 0


def attention_ffn_program(nc, a):
    N, S, E = a["x"].shape
    D = E // 2
    H = 16
    DH = D // H
    HP = H // 2
    NT = S // P
    NH = S // BANK
    TPH = BANK // P
    NG = H // 4
    ROWS = DH * len(TERMS)
    MROWS = 3
    SCALE = 1.0 / float(E // H) ** 0.5
    assert (S, E, DH, NH) == (1024, 256, 8, 2)

    x_dram = a["x"].rearrange("n (p t) e -> n p t e", p=P)
    out_dram = a["out"].rearrange("n (p t) e -> n p t e", p=P)

    with ExitStack() as ctx:
        def sb(name, shape, dt=F32):
            return ctx.enter_context(nc.sbuf_tensor(name, shape, dt))

        def counter(name):
            return Counter(ctx.enter_context(nc.semaphore(name)))

        scoresT_ps = ctx.enter_context(nc.psum_tensor("scoresT_ps", [P, 4 * BANK], F32))
        max_ps = ctx.enter_context(nc.psum_tensor("max_ps", [P, 2 * BANK], F32))
        heads_ps = ctx.enter_context(nc.psum_tensor("heads_ps", [P, BANK], F32))
        misc_ps = ctx.enter_context(nc.psum_tensor("misc_ps", [P, BANK], F32))

        XS = 2
        x_in = sb("x_in", [P, NT, E])
        x_sb = sb("x_sb", [P, XS, NT, E])
        q_rows = sb("q_rows", [P, 2, HP, S], BF16)
        k_rows = sb("k_rows", [P, 2, HP, S], BF16)
        q_pad = sb("q_pad", [P, 2, 2, 2, BANK], BF16)
        q_pad_max = sb("q_pad_max", [P, 2, 2, BANK], BF16)
        v_sb = sb("v_sb", [P, 2, NT, H, DH + 2])
        NP = 2
        p_sb = sb("p_sb", [P, NP, 4, BANK])
        couple = sb("couple", [P, 4, BANK])
        headsT = sb("headsT", [P, NH, NG, BANK])
        parts = sb("parts", [P, 2, 3, S], BF16)
        tok = sb("tok", [P, NT, D])
        feat = sb("feat", [P, S])
        y_sb = sb("y_sb", [P, NT, E])
        y_flat = y_sb[:, :, :].rearrange("p t e -> p (t e)")
        proj_sb = [y_flat[:, 0:BANK], y_flat[:, BANK:2 * BANK]]
        rest_sb = [y_flat[:, 2 * BANK:3 * BANK], y_flat[:, 3 * BANK:4 * BANK]]
        state = sb("state", [P, 2, S])
        wq, wk, wv = sb("wq", [P, D]), sb("wk", [P, D]), sb("wv", [P, D])
        wo = sb("wo", [P, E])
        bo = sb("bo", [P, E])
        w1, w2, w3 = sb("w1", [P, 2, E]), sb("w2", [P, 2, D]), sb("w3", [P, D // 2])
        g1, g2 = sb("g1", [P, 2, D]), sb("g2", [P, D // 2])
        b1, b2, b3 = sb("b1", [P, 2]), sb("b2", [P, 1]), sb("b3", [D // 2, 1])
        gb1, gb2 = sb("gb1", [P, 1]), sb("gb2", [D // 2, 1])
        w4, g3 = sb("w4", [D // 2, 1]), sb("g3", [D // 2, 1])
        w4_all, g3_all = sb("w4_all", [D // 2, P]), sb("g3_all", [D // 2, P])
        b4, gb3, ar = sb("b4", [P, 1]), sb("gb3", [P, 1]), sb("ar", [P, 1])
        b4_half, gb3_half = sb("b4_half", [P, 1]), sb("gb3_half", [P, 1])
        ones = sb("ones", [D // 2, P])
        ident = sb("ident", [P, P])
        sign = sb("sign", [P, 1])
        tenth = sb("tenth", [P, 1])
        ar_token = sb("ar_token", [P, 1])
        ar_global = sb("ar_global", [P, 1])
        shift = sb("shift", [P, 1])
        MU = 2 * 2 * TPH
        max_parts = sb("max_parts", [P, 2, 2, MU])
        max_all = sb("max_all", [P, MU])
        max_rest = sb("max_rest", [P, MU])
        max_split = sb("max_split", [P, 2 * 2, MROWS, TPH], BF16)
        neg_rows = sb("neg_rows", [MROWS * MU, P], BF16)
        ident_bf = sb("ident_bf", [P, P], BF16)
        stats = sb("stats", [P, NT, 6])
        moments = sb("moments", [P, NT, 2])
        rstd = sb("rstd", [P, NT])
        offset = sb("offset", [P, NT])
        minus_half = sb("minus_half", [P, NT])
        recip = sb("recip", [P, H])
        sums = sb("sums", [P, 2, NH])
        mean_g = sb("mean_g", [P, 2])
        hg1, hg2, tg = sb("hg1", [P, 1]), sb("hg2", [D // 2, 1]), sb("tg", [P, 1])

        c_w = counter("weights_loaded")
        c_xin = counter("x_in_loaded")
        c_x = [counter(f"x_loaded{i}") for i in range(XS)]
        c_out = [counter(f"out_stored{i}") for i in range(XS)]
        c_rows = [[counter(f"rows_laid{i}_{part}") for part in ("k_and_q0", "q1")] for i in range(2)]
        c_mrows = counter("max_rows_laid")
        c_set = counter("constants_set")
        c_set_p = counter("constants_pool")
        c_st = counter("scoresT_done")
        c_pv = counter("pv_done")
        c_mm = counter("max_scores_done")
        c_mi = counter("misc_mm_done")
        c_ff = counter("ffn_mm_done")
        c_exp = counter("exp_done")
        c_act = counter("act_misc_done")
        c_red = counter("max_taken")
        c_dve = counter("dve_misc_done")
        c_pool = counter("pool_done")
        c_pad = counter("q_padded")
        c_pad_a = counter("q_padded_act")

        pe, act, dve, pool, sp = Queue(), Queue(), Queue(), Queue(), Queue()

        def load(dst, src):
            return sp.do(lambda e: e.dma_start(dst, src), c_w, 16)

        def load_x_in(b, *free):
            sp.wait(*free)
            loaded_in[b] = sp.do(lambda e: e.dma_start(x_in[:, :, :], x_dram[b]), c_xin, 16)

        def load_x(b):
            slot = b % XS
            if b >= XS:
                sp.wait(stored[b - XS])
            loaded[b] = sp.do(lambda e: e.dma_start(x_sb[:, slot, :, :], x_dram[b]), c_x[slot], 16)

        loaded_in, loaded, stored = {}, {}, {}
        load_x_in(0)
        load(wq[:, :], a["wq_t"])
        load(wk[:, :], a["wk_t"])
        load(wv[:, :], a["wv_t"])
        load(wo[:, :], a["wo_t"])
        load(bo[:, :], a["bo"].partition_broadcast(P))
        load(w1[:, :, :], a["w1"].rearrange("(k p) n -> p k n", p=P))
        load(w2[:, :, :], a["w2"].rearrange("(k p) n -> p k n", p=P))
        load(w3[:, :], a["w3"])
        load(w4[:, :], a["w4"])
        load(g1[:, :, :], a["g1"].rearrange("(k p) n -> p k n", p=P))
        load(g2[:, :], a["g2"])
        load(g3[:, :], a["g3"])
        for k in range(2):
            load(b1[:, k:k + 1], a["b1"][k * P:(k + 1) * P].rearrange("(p k) -> p k", k=1))
        load(b2[:, :], a["b2"].rearrange("(p k) -> p k", k=1))
        load(b3[:, :], a["b3"].rearrange("(p k) -> p k", k=1))
        load(gb1[:, :], a["gb1"].rearrange("(p k) -> p k", k=1))
        load(gb2[:, :], a["gb2"].rearrange("(p k) -> p k", k=1))
        load(b4[:, :], a["b4"].partition_broadcast(P))
        load(gb3[:, :], a["gb3"].partition_broadcast(P))
        weights = load(ar[:, :], a["ar"].partition_broadcast(P))

        m = pool.do(lambda e: e.memset(ident[:, :], 0.0), c_set_p)
        pool.wait(m)
        ident_set = pool.do(lambda e: e.affine_select(
            out=ident[:, :], in_=ident[:, :], compare_op=ALU.not_equal, fill=1.0, base=0,
            pattern=[[-1, P]], channel_multiplier=1), c_set_p)
        pool.wait(ident_set)
        pool.do(lambda e: e.tensor_copy(ident_bf[:, :], ident[:, :]), c_set_p)
        m = pool.do(lambda e: e.memset(minus_half[:, :], -0.5), c_set_p)
        m = pool.do(lambda e: e.memset(v_sb[:, :, :, :, DH:DH + 1], 1.0), c_set_p)
        ones_rows = lambda side: k_rows[64 * side + 32:64 * side + 64, :, :, :].rearrange(
            "p s h n -> p (s h n)").bitcast(F32)
        pool.wait(m)
        rows_set = pool.do(lambda e: e.memset(ones_rows(0), TWO_ONES), c_set_p)
        pool.wait(rows_set)
        sp.wait(rows_set)
        pe.wait(ident_set, weights)

        dve.do(lambda e: e.memset(sign[0:D // 2, :], 1.0))
        dve.do(lambda e: e.memset(sign[D // 2:D, :], -1.0))
        dve.do(lambda e: e.memset(q_pad[:, :, :, :, :], 0.0))
        dve.do(lambda e: e.memset(q_pad_max[:, :, :, :], 0.0))
        dve.do(lambda e: e.memset(heads_ps[:, :], 0.0))
        ones_set = dve.do(lambda e: e.memset(ones[:, :], 1.0), c_set)

        def set_rows():
            sp.wait(dve.do(lambda e: e.memset(ones_rows(1), TWO_ONES), c_set))

        def derive_constants():
            dve.wait(ones_set, weights)
            dve.do(lambda e: e.tensor_scalar(w4_all[:, :], ones[:, :], w4[:, 0:1], None, ALU.mult))
            dve.do(lambda e: e.tensor_scalar(g3_all[:, :], ones[:, :], g3[:, 0:1], None, ALU.mult))
            dve.do(lambda e: e.tensor_scalar(b4_half[:, :], b4[:, :], 0.5, None, ALU.mult))
            dve.do(lambda e: e.tensor_scalar(gb3_half[:, :], gb3[:, :], 0.5, None, ALU.mult))
            dve.do(lambda e: e.tensor_scalar(tenth[:, :], sign[:, :], 0.1, None, ALU.mult))
            dve.do(lambda e: e.tensor_scalar(ar_token[:, :], sign[:, :], ar[:, 0:1], 0.3, ALU.mult, ALU.mult))
            derived = dve.do(lambda e: e.tensor_scalar(ar_global[:, :], sign[:, :], ar[:, 0:1], 0.7,
                                                       ALU.mult, ALU.mult), c_set)
            heads_free[0] = derived
            pe.wait(derived, rows_set)
            act.wait(derived)
            pool.wait(derived)

        st = dict(tok=None, feat=None, y=None, state=None, proj=[None, None], rest=[None, None],
                  mom=[(), ()], recip=None, max_split=None, max_split_read=None, neg_rows_read=None)
        st.update({bank: None for bank in range(4)})
        exp_mark, pv_mark, heads_evac = {}, {}, {}
        headsT_read = {}
        rows_laid, mrows_laid = {}, {}
        v_ready, v_read = {}, {}
        main_end = {}

        def pause(n):
            for _ in range(n):
                yield

        banks = [misc_ps[:, :], max_ps[:, 0:BANK], max_ps[:, BANK:2 * BANK], heads_ps[:, :]]
        MISC, MAX, HEADS = 0, (1, 2), 3
        rotation = [MISC, *MAX]

        def misc_job(emits):
            rotation.append(rotation.pop(0))
            bank = rotation[-1]
            pe.wait(st[bank])
            for f in emits[:-1]:
                pe.do(lambda e, f=f: f(e, banks[bank]))
            return bank, pe.do(lambda e: emits[-1](e, banks[bank]), c_mi)

        def row_stats(src, ready, blocks=range(NT), every=2):
            of = slice(blocks[0], blocks[-1] + 1)
            dve.wait(ready)
            for half in {t // TPH for t in blocks}:
                dve.wait(*st["mom"][half])
            for t in blocks:
                m = dve.do(lambda e, t=t: e.bn_stats(stats[:, t, :], src(t)), c_dve)
                yield from pause(every)
            dve.wait(m)
            for t in blocks:
                m = dve.do(lambda e, t=t: e.bn_aggr(moments[:, t, :], stats[:, t, :]), c_dve)
            pool.wait(m)
            m = pool.do(lambda e: e.tensor_scalar(rstd[:, of], moments[:, of, 1], EPS, None, ALU.add), c_pool)
            pool.wait(m)
            m = pool.do(lambda e: e.tensor_tensor(rstd[:, of], rstd[:, of], minus_half[:, of], ALU.pow), c_pool)
            m = pool.do(lambda e: e.tensor_scalar(offset[:, of], moments[:, of, 0], -1.0, None, ALU.mult), c_pool)
            pool.wait(m)
            return pool.do(lambda e: e.tensor_tensor(offset[:, of], offset[:, of], rstd[:, of], ALU.mult), c_pool)

        def normalize(dst, src, ready, *free, blocks=range(NT), late=False):
            helper, c_helper, every = (dve, c_dve, 2) if late else (pool, c_pool, 3)
            helper.wait(ready, *free)
            act.wait(ready, *free)
            for t in blocks:
                if t % every == 0:
                    mp = helper.do(lambda e, t=t: e.tensor_scalar(dst(t), src(t), moments[:, t, 0:1], rstd[:, t:t + 1],
                                                                  ALU.subtract, ALU.mult), c_helper)
                else:
                    ma = act.do(lambda e, t=t: e.activation(dst(t), src(t), ACT.Identity, bias=offset[:, t:t + 1],
                                                            scale=rstd[:, t:t + 1]), c_act)
                    yield
            for half in {t // TPH for t in blocks}:
                st["mom"][half] = [mp, ma]
            return [mp, ma]

        def add_to(xb, y, ready, late):
            adder, c_adder = (dve, c_dve) if late else (pool, c_pool)
            adder.wait(*ready)
            return adder.do(lambda e: e.tensor_tensor(xb, xb, y, ALU.add), c_adder)

        def project_qk(b):
            ready = yield from row_stats(lambda t: x_in[:, t, :], loaded_in[b], every=2 if b > 1 else 1)
            yield from pause(3)
            ready = yield from normalize(lambda t: tok[:, t, :], lambda t: x_in[:, t, 0:D], ready, st["tok"])
            if b + 1 < N:
                load_x_in(b + 1, *ready)
            for h in range(NH):
                pe.wait(*ready)
                bank, m = misc_job([lambda e, ps, t=t: e.transpose(ps[:, t % TPH * P:(t % TPH + 1) * P], tok[:, t, :],
                                                         ident[:, :]) for t in range(h * TPH, (h + 1) * TPH)])
                st["tok"] = m
                act.wait(m, st["feat"])
                st[bank] = feat_ready = act.do(lambda e, ps=banks[bank], h=h: e.activation(
                    feat[:, h * BANK:(h + 1) * BANK], ps[:, :], ACT.Copy), c_act)
                yield from pause(2)
            splitter, c_split = (dve, c_dve) if b == 0 else (pool, c_pool)
            for i, w in enumerate((wq, wk)):
                for h in range(NH):
                    cols = slice(h * BANK, (h + 1) * BANK)
                    pe.wait(feat_ready)
                    bank, m = misc_job([lambda e, ps, w=w, c=cols: e.matmul(ps[:, :], w[:, :], feat[:, c],
                                                                  start=True, stop=True)])
                    st["feat"] = m
                    hi, mid, lo = (parts[:, i, j, cols] for j in range(3))
                    proj, rest = proj_sb[h], rest_sb[h]
                    act.wait(m, st["proj"][h], st["y"], *rows_laid.get(b - 1, ()))
                    got = act.do(lambda e, ps=banks[bank], proj=proj: e.activation(proj, ps[:, :], ACT.Copy), c_act)
                    st[bank] = got = act.do(lambda e, ps=banks[bank], hi=hi: e.activation(hi, ps[:, :], ACT.Copy), c_act)
                    splitter.wait(got, st["rest"][h])
                    m = splitter.do(lambda e, hi=hi, proj=proj, rest=rest: e.tensor_tensor(rest, proj, hi,
                                                                                           ALU.subtract), c_split)
                    st["proj"][h] = m
                    yield from pause(3)
                    dve.wait(m)
                    m = dve.do(lambda e, mid=mid, rest=rest: e.tensor_copy(mid, rest), c_dve)
                    splitter.wait(m)
                    st["rest"][h] = parts_ready = splitter.do(
                        lambda e, mid=mid, lo=lo, rest=rest: e.tensor_tensor(lo, rest, mid, ALU.subtract), c_split)
                    yield
            st["y"] = parts_ready
            return feat_ready, parts_ready

        def lay_rows(b, parts_ready, *free):
            slot = b % 2
            sp.wait(parts_ready, *free)
            for last, todo in enumerate((((1, 0), (1, 1), (0, 0)), ((0, 1),))):
                for i, side in todo:
                    rows = (q_rows, k_rows)[i]
                    for n, term in enumerate(TERMS):
                        at = 64 * side + DH * n
                        m = sp.do(lambda e, i=i, s=side, at=at, part=term[i], rows=rows: e.dma_start(
                            rows[at:at + DH, slot, :, :], parts[64 * s:64 * s + 64, i, part, :]), c_rows[slot][last],
                            16)
                rows_laid.setdefault(b, []).append(m)

        def project_v(b, feat_ready, *free):
            for h in range(NH):
                pe.wait(feat_ready)
                bank, m = misc_job([lambda e, ps, t=t: e.matmul(ps[:, t % TPH * P:(t % TPH + 1) * P],
                                                      feat[:, t * P:(t + 1) * P], wv[:, :], start=True, stop=True)
                              for t in range(h * TPH, (h + 1) * TPH)])
                st["feat"] = m
                act.wait(m, *free)
                v_ready[b] = st[bank] = act.do(lambda e, ps=banks[bank], h=h: e.activation(
                    v_sb[:, b % 2, h * TPH:(h + 1) * TPH, :, 0:DH],
                    ps[:, :].rearrange("p (t h d) -> p t h d", t=TPH, h=H), ACT.Copy), c_act)
                yield

        def divide_heads(b, h):
            for t in range(h * TPH, (h + 1) * TPH):
                cols = slice(t % TPH * P, (t % TPH + 1) * P)
                pe.wait(heads_evac[b, h])
                bank, m = misc_job([lambda e, ps, g=g, c=cols: e.transpose(ps[:, g * P:(g + 1) * P], headsT[:, h, g, c],
                                                                 ident[:, :]) for g in range(NG)])
                headsT_read[b, h] = m
                by_head = banks[bank][:, :].rearrange("p (h c) -> p h c", h=H)
                dve.wait(m, st["recip"])
                m = dve.do(lambda e, v=by_head: e.reciprocal(recip[:, :], v[:, :, DH]), c_dve)
                dve.wait(m, st["tok"])
                st[bank] = st["recip"] = done = dve.do(lambda e, t=t, v=by_head: e.tensor_tensor(
                    tok[:, t, :].rearrange("p (h d) -> p h d", h=H), v[:, :, 0:DH],
                    recip[:, :].unsqueeze(2).to_broadcast([P, H, DH]), ALU.mult), c_dve)
                divided[b, h] = done
                yield from pause(2)

        divided = {}

        def project_out(b):
            xb = x_sb[:, b % XS, :, :]
            late = b == N - 1
            for h in range(NH):
                pe.wait(divided[b, h])
                bank, m = misc_job([lambda e, ps, t=t: e.transpose(ps[:, t % TPH * P:(t % TPH + 1) * P], tok[:, t, :],
                                                         ident[:, :]) for t in range(h * TPH, (h + 1) * TPH)])
                st["tok"] = m
                act.wait(m, st["feat"])
                st[bank] = feat_ready = act.do(lambda e, ps=banks[bank], h=h: e.activation(
                    feat[:, h * BANK:(h + 1) * BANK], ps[:, :], ACT.Copy), c_act)
                yield from pause(2)
            for t in range(0, NT, 2):
                pe.wait(feat_ready)
                bank, m = misc_job([lambda e, ps, t=t, u=u: e.matmul(ps[:, u * E:(u + 1) * E],
                                                           feat[:, (t + u) * P:(t + u + 1) * P], wo[:, :],
                                                           start=True, stop=True) for u in range(2)])
                st["feat"] = m
                dve.wait(m, st["y"])
                st[bank] = y_ready = dve.do(lambda e, ps=banks[bank], t=t: e.tensor_tensor(
                    y_sb[:, t:t + 2, :], ps[:, :].rearrange("p (u e) -> p u e", u=2),
                    bo[:, :].unsqueeze(1).to_broadcast([P, 2, E]), ALU.add), c_dve)
                yield from pause(2)
            ready = yield from row_stats(lambda t: y_sb[:, t, :], y_ready)
            yield from pause(3)
            ready = yield from normalize(lambda t: y_sb[:, t, :], lambda t: y_sb[:, t, :], ready,
                                         late=late)
            ready = add_to(xb, y_sb[:, :, :], [*ready, loaded[b]], late)
            yield from pause(8)
            ready = yield from row_stats(lambda t: xb[:, t, :], ready)
            yield from pause(3)
            ready = yield from normalize(lambda t: y_sb[:, t, :], lambda t: xb[:, t, :], ready, late=late)
            normalized[b] = ready

        normalized = {}

        def transpose_state(b):
            ready = normalized[b]
            for half in range(2):
                for h in range(NH):
                    pe.wait(*ready)
                    bank, m = misc_job([lambda e, ps, t=t, f=half: e.transpose(
                        ps[:, t % TPH * P:(t % TPH + 1) * P], y_sb[:, t, f * P:(f + 1) * P], ident[:, :])
                        for t in range(h * TPH, (h + 1) * TPH)])
                    st["y"] = m
                    act.wait(m, st["state"], g_read.get(b - 1))
                    st[bank] = state_ready[b] = act.do(lambda e, ps=banks[bank], f=half, h=h: e.activation(
                        state[:, f, h * BANK:(h + 1) * BANK], ps[:, :], ACT.Copy,
                        accum_out=sums[:, f, h:h + 1]), c_act)
                    yield from pause(2)

        state_ready, g_read, updated = {}, {}, {}

        def finish(b, y_sb, last_use, blocks=range(NT)):
            slot, late = b % XS, b >= N - 2
            of = slice(blocks[0], blocks[-1] + 1)
            for t in blocks[::2]:
                pe.wait(*updated[b, t // TPH])
                bank, m = misc_job([lambda e, ps, t=t, u=u, f=f: e.transpose(
                    ps[:, u * E + f * P:u * E + (f + 1) * P], state[:, f, (t + u) * P:(t + u + 1) * P], ident[:, :])
                    for u in range(2) for f in range(2)])
                st["state"] = m
                act.wait(m, *last_use)
                st[bank] = y_ready = act.do(lambda e, ps=banks[bank], t=t: e.activation(
                    y_sb[:, t:t + 2, :], ps[:, :].rearrange("p (u e) -> p u e", u=2), ACT.Copy), c_act)
                yield from pause(2)
            ready = yield from row_stats(lambda t: y_sb[:, t, :], y_ready, blocks)
            yield from pause(3)
            ready = yield from normalize(lambda t: y_sb[:, t, :], lambda t: y_sb[:, t, :], ready, blocks=blocks,
                                         late=late)
            st["y"] = ready = add_to(x_sb[:, slot, of, :], y_sb[:, of, :], ready, late)
            sp.wait(ready)
            stored[b] = sp.do(lambda e: e.dma_start(out_dram[b][:, of, :], x_sb[:, slot, of, :]), c_out[slot], 16)
            yield

        def copy_rows(dst, src, on_act, *ready):
            if on_act:
                act.wait(*ready)
                return act.do(lambda e: e.activation(dst, src, ACT.Copy), c_pad_a)
            dve.wait(*ready)
            return dve.do(lambda e: e.tensor_copy(dst, src), c_pad)

        def maxima(b):
            slot = b % 2
            if b == 0:
                rotation[:] = [MISC]
                reduced.update({n: st[bank] for n, bank in enumerate(MAX)})
            sides = [(h, g, side) for h in range(NH) for g in range(NG) for side in range(2)]

            def pad(h, g, side):
                rows = slice(64 * side, 64 * side + ROWS)
                return copy_rows(q_pad_max[rows, side, :, :], q_rows[rows, slot, 2 * g:2 * g + 2, h * BANK:(h + 1) * BANK],
                                 b < 2, rows_laid[b][side], pad_read.get(side))

            ahead = pad(*sides[0])
            for i, (h, g, side) in enumerate(sides):
                ready, u = ahead, (h * NG + g) % 2
                if i + 1 < len(sides):
                    ahead = pad(*sides[i + 1])
                if side == 0:
                    dve.wait(max_parts_read.get(u))
                n = 0
                for two in range(2):
                    for qb in range(TPH):
                        for kh in range(NH):
                            bank = max_ps[:, n % 2 * BANK:(n % 2 + 1) * BANK]
                            pe.wait(ready, reduced.get(n % 2))
                            pad_read[side] = m = pe.do(lambda e, bank=bank, s=side, t=two, q=qb, k=kh, p=2 * g + two:
                                                       e.matmul(bank, q_pad_max[:, s, t, q * P:(q + 1) * P],
                                                                k_rows[:, slot, p, k * BANK:(k + 1) * BANK],
                                                                start=True, stop=True), c_mm)
                            dve.wait(m)
                            col = (side * 2 + two) * TPH + qb
                            reduced[n % 2] = dve.do(lambda e, bank=bank, k=kh, c=col, u=u: e.tensor_reduce(
                                max_parts[:, u, k, c:c + 1], bank, AX.X, ALU.max), c_red)
                            n += 1
                            if side == 1 and n == 2 * TPH * NH:
                                stream["laying"] = lay_maxima(b, h, g, reduced[(n - 1) % 2])
                                next(stream["laying"])
                            yield

        stream = dict(batch=0, units=None, laying=None, count=0)

        def take_maxima(n):
            for _ in range(n):
                if stream["laying"] is not None and next(stream["laying"], "end") == "end":
                    stream["laying"] = None
                b = stream["batch"]
                if stream["units"] is None and b < N and b in rows_laid:
                    stream["units"] = maxima(b)
                if stream["units"] is not None:
                    next(stream["units"])
                    stream["count"] += 1
                    if stream["count"] == (b + 1) * PER_BATCH:
                        stream["units"] = None
                        stream["batch"] += 1

        PER_GROUP = 2 * 2 * TPH * NH
        PER_BATCH = PER_GROUP * NH * NG
        SPLIT_TIME = 4
        reduced, pad_read, max_parts_read = {}, {}, {}

        def lay_maxima(b, h, g, ready):
            u = (h * NG + g) % 2
            dve.wait(ready, st["max_split"])
            max_parts_read[u] = m = dve.do(lambda e: e.tensor_tensor(
                max_all[:, :], max_parts[:, u, 0, :], max_parts[:, u, 1, :], ALU.max), c_dve)
            by_head = lambda tile: tile[:, :].rearrange("p (s q) -> p s q", q=TPH)
            hi, mid, lo = (max_split[:, :, j, :] for j in range(MROWS))
            pool.wait(m, st["max_split_read"])
            m = pool.do(lambda e: e.tensor_copy(hi, by_head(max_all)), c_pool)
            pool.wait(m)
            m = pool.do(lambda e: e.tensor_tensor(by_head(max_rest), by_head(max_all), hi, ALU.subtract), c_pool)
            pool.wait(m)
            m = pool.do(lambda e: e.tensor_copy(mid, by_head(max_rest)), c_pool)
            pool.wait(m)
            st["max_split"] = m = pool.do(lambda e: e.tensor_tensor(lo, by_head(max_rest), mid, ALU.subtract), c_pool)
            for _ in range(SPLIT_TIME):
                yield
            pe.wait(m)
            bank, m = misc_job([lambda e, ps: e.matmul(
                ps[0:MU * MROWS, 0:P], max_split[:, :, :, :].rearrange("p s j q -> p (s j q)"), ident_bf[:, :],
                start=True, stop=True)])
            st["max_split_read"] = m
            act.wait(m, st["neg_rows_read"])
            st[bank] = m = act.do(lambda e, ps=banks[bank]: e.activation(neg_rows[:, :], ps[0:MU * MROWS, 0:P], ACT.Copy,
                                                           scale=-1.0), c_act)
            sp.wait(m, main_end.get(b - 2))
            for side in range(2):
                for two in range(2):
                    at, n = 64 * side + ROWS, MROWS * TPH * (2 * side + two)
                    m = sp.do(lambda e, at=at, n=n, p=2 * g + two: e.dma_start(
                        q_rows[at:at + MROWS, b % 2, p, h * BANK:(h + 1) * BANK],
                        neg_rows[n:n + MROWS * TPH, :]), c_mrows, 16)
            st["neg_rows_read"] = mrows_laid[b, h, g] = m

        step_no = [0]
        LAY_TIME = 16
        PAD_AT = 5

        def needed(b, group):
            return min(b * PER_BATCH + (group + 1) * PER_GROUP + LAY_TIME, N * PER_BATCH)

        def pace(b, pieces):
            group, piece = divmod(pieces - 1 + 3 * (NT - PAD_AT), 3 * NT)
            return max(1, -(-(needed(b, group + 1) - stream["count"]) // (3 * NT - piece)))

        def pad_unit(b, h, g):
            u = (h * NG + g) % 2
            while stream["count"] < needed(b, h * NG + g) and stream["batch"] in rows_laid:
                take_maxima(1)
            while (b, h, g) not in mrows_laid:
                take_maxima(1)
            padded[b, h, g] = []
            for side in range(2):
                rows = slice(64 * side, 64 * side + ROWS + MROWS)
                padded[b, h, g].append(copy_rows(
                    q_pad[rows, u, side, :, :], q_rows[rows, b % 2, 2 * g:2 * g + 2, h * BANK:(h + 1) * BANK],
                    b == 0, *rows_laid[b], mrows_laid[b, h, g], unit_read.get((0, u))))

        padded = {}

        def attention_steps(b):
            slot = b % 2
            todo = [(h, g, kb) for h in range(NH) for g in range(NG) for kb in range(NT)]
            last = None

            def scores(n, h, g, kb, two):
                pair = 2 * g + two
                pe.wait(*padded[b, h, g], exp_mark.get((n - 1, two)), ffn_banks[0])
                for side in range(2):
                    bank = scoresT_ps[:, (2 * two + side) * BANK:(2 * two + side + 1) * BANK]
                    f = lambda e, s=side, bank=bank: e.matmul(
                        bank, k_rows[:, slot, pair, kb * P:(kb + 1) * P], q_pad[:, (h * NG + g) % 2, s, two, :],
                        start=True, stop=True)
                    m = pe.do(f, c_st if side else None)
                unit_read[0, (h * NG + g) % 2] = m
                act.wait(m, pv_mark.get(n - NP), ffn_temps[0])
                exp_mark[n, two] = act.do(lambda e: e.activation(
                    p_sb[:, n % NP, 2 * two:2 * two + 2, :].rearrange("p h n -> p (h n)"),
                    scoresT_ps[:, 2 * two * BANK:(2 * two + 2) * BANK], ACT.Exp, scale=SCALE), c_exp)

            def weigh(n, h, g, kb):
                pe.wait(exp_mark[n, 0], exp_mark[n, 1], v_ready[b])
                if kb == 0:
                    pe.wait(heads_free[0])
                for j in range(4):
                    f = lambda e, j=j: e.matmul(
                        heads_ps[32 * j:32 * j + DH + 1, :], v_sb[:, slot, kb, 4 * g + j, 0:DH + 1],
                        p_sb[:, n % NP, j, :], start=(kb == 0), stop=(kb == NT - 1))
                    m = pe.do(f, c_pv if j == 3 else None)
                pv_mark[n] = m
                if kb == NT - 1:
                    act.wait(m, headsT_read.get((b - 1, h)))
                    heads_free[0] = heads_evac[b, h] = act.do(lambda e: e.activation(
                        headsT[:, h, g, :], heads_ps[:, :], ACT.Copy), c_act)

            units = [(b, h, g) for h in range(NH) for g in range(NG)] + [(b + 1, 0, 0)]
            if (b, 0, 0) not in padded:
                pad_unit(b, 0, 0)
            for h, g, kb in todo:
                if kb == PAD_AT:
                    nxt = units[h * NG + g + 1]
                    if nxt[0] in rows_laid:
                        pad_unit(*nxt)
                n = step_no[0]
                step_no[0] += 1
                scores(n, h, g, kb, 0)
                yield "piece"
                scores(n, h, g, kb, 1)
                yield "piece"
                if last:
                    weigh(*last)
                last = (n, h, g, kb)
                yield "step"
            weigh(*last)
            main_end[b] = pv_mark[last[0]]

        unit_read = {}
        heads_free, ffn_banks, ffn_temps = [None], [None], [None]

        def coupling(b):
            h1 = lambda c, m: p_sb[:, 0, 2 * c + m, :]
            h2 = lambda c: p_sb[:, 1, c, :]
            h3 = lambda c: p_sb[0:D // 2, 1, 2 + c, :]
            tf = lambda c: couple[:, c, :]
            twist_a, twist_b = couple[:, 2, :], couple[:, 3, :]
            bank = lambda c, i: scoresT_ps[:, (2 * c + i) * BANK:(2 * c + i + 1) * BANK]
            n = step_no[0] - 1
            before = [main_end.get(b + 1), exp_mark.get((n, 0)), exp_mark.get((n, 1))]
            pe.wait(*before)
            act.wait(*before)
            pool.wait(*before)
            dve.wait(*before)
            cols = [slice(c * BANK, (c + 1) * BANK) for c in range(NH)]
            ready = {c: [state_ready[b]] for c in range(NH)}
            tw = [None, None]
            gl = global_net(b)
            next(gl)
            hidden, scaled = {}, {}

            def first(c, m):
                pe.wait(*ready[c])
                for k in range(2):
                    mk = matmul(bank(c, m), w1[:, k, m * P:(m + 1) * P], state[:, k, cols[c]], k, 2)
                    if k == 0:
                        yield
                hidden[c] = gelu(h1(c, m), bank(c, m), b1[:, m:m + 1], mk)

            def second(c):
                pe.wait(hidden[c])
                for k in range(2):
                    mk = matmul(bank(c, 0), w2[:, k, :], h1(c, k), k, 2)
                    if k == 0:
                        yield
                hidden[c] = gelu(h2(c), bank(c, 0), b2[:, 0:1], mk)

            def third(c):
                pe.wait(hidden[c])
                mk = matmul(bank(c, 1)[0:D // 2, :], w3[:, :], h2(c), 0, 1)
                hidden[c] = gelu(h3(c), bank(c, 1)[0:D // 2, :], b3[:, 0:1], mk)
                return
                yield

            def fourth(c):
                pe.wait(hidden[c])
                mk = matmul(bank(c, 0), w4_all[:, :], h3(c), 0, 1)
                act.wait(mk, *(last_tf.get(c) or ()))
                wrote = act.do(lambda e: e.activation(tf(c), bank(c, 0), ACT.Tanh, bias=b4_half[:, 0:1],
                                                      scale=0.5), c_act)
                ffn_banks[0] = wrote
                ffn_temps[0] = mk
                act.wait(wrote, shift_ready[b])
                cs = act.do(lambda e: e.activation(tf(c), tf(c), ACT.Identity, bias=shift[:, 0:1],
                                                   scale=ar_token[:, 0:1]), c_act)
                scaled[c] = cs
                return
                yield

            def twist(c):
                pool.wait(scaled[c], tw[0])
                t1 = pool.do(lambda e: e.tensor_tensor(twist_a, tf(c), state[:, 1, cols[c]], ALU.mult), c_pool)
                dve.wait(scaled[c], tw[1])
                t2 = dve.do(lambda e: e.tensor_tensor(twist_b, tf(c), state[:, 0, cols[c]], ALU.mult), c_dve)
                last_tf[c] = [t1, t2]

            def update(c):
                A, B = state[:, 0, cols[c]], state[:, 1, cols[c]]
                pool.wait(*last_tf[c])
                u1 = pool.do(lambda e: e.tensor_tensor(A, A, twist_a, ALU.add), c_pool)
                dve.wait(*last_tf[c])
                u2 = dve.do(lambda e: e.tensor_tensor(B, B, twist_b, ALU.subtract), c_dve)
                tw[:] = [u1, u2]
                ready[c] = [u1, u2]

            def matmul(out, lhs, rhs, k, of):
                return pe.do(lambda e: e.matmul(out, lhs, rhs, start=(k == 0), stop=(k == of - 1)),
                             c_ff if k == of - 1 else None)

            def gelu(dst, src, bias, mk):
                act.wait(mk)
                return act.do(lambda e: e.activation(dst, src, ACT.Gelu, bias=bias), c_act)

            for cycle in range(3):
                for layer, room, half, step in (
                        (first(0, 0), 1, 1, update), (first(0, 1), 1, 0, None), (first(1, 0), 1, 0, None),
                        (second(0), 2, 0, None), (first(1, 1), 2, 0, None), (third(0), 1, 0, None),
                        (second(1), 1, 0, None), (fourth(0), 2, 0, None), (third(1), 2, 0, twist),
                        (fourth(1), 1, 0, update), (nothing(), 2, 1, twist)):
                    for _ in layer:
                        yield 1
                    yield room
                    if step and half in scaled:
                        step(half)
                    next(gl, None)
            update(1)
            for c in range(NH):
                updated[b, c] = ready[c]

        last_tf, shift_ready = {}, {}

        def global_net(b):
            dve.wait(state_ready[b])
            m = dve.do(lambda e: e.tensor_tensor(mean_g[:, :], sums[:, :, 0], sums[:, :, 1], ALU.add), c_dve)
            dve.wait(m)
            g_read[b] = m
            m = dve.do(lambda e: e.tensor_scalar(mean_g[:, :], mean_g[:, :], 1.0 / S, None, ALU.mult), c_dve)
            yield
            pe.wait(m)
            bank, m = misc_job([lambda e, ps, k=k: e.matmul(ps[:, 0:1], g1[:, k, :], mean_g[:, k:k + 1], start=(k == 0),
                                                  stop=(k == 1)) for k in range(2)])
            act.wait(m)
            st[bank] = m = act.do(lambda e, ps=banks[bank]: e.activation(hg1[:, :], ps[:, 0:1], ACT.Gelu, bias=gb1[:, 0:1]), c_act)
            yield
            pe.wait(m)
            bank, m = misc_job([lambda e, ps: e.matmul(ps[0:D // 2, 0:1], g2[:, :], hg1[:, :], start=True, stop=True)])
            act.wait(m)
            st[bank] = m = act.do(lambda e, ps=banks[bank]: e.activation(hg2[:, :], ps[0:D // 2, 0:1], ACT.Gelu,
                                                           bias=gb2[:, 0:1]), c_act)
            yield
            pe.wait(m)
            bank, m = misc_job([lambda e, ps: e.matmul(ps[:, 0:1], g3_all[:, :], hg2[:, :], start=True, stop=True)])
            act.wait(m)
            st[bank] = m = act.do(lambda e, ps=banks[bank]: e.activation(tg[:, :], ps[:, 0:1], ACT.Tanh, bias=gb3_half[:, 0:1],
                                                           scale=0.5), c_act)
            pool.wait(m)
            shift_ready[b] = pool.do(lambda e: e.tensor_scalar(shift[:, :], tg[:, :], ar_global[:, 0:1], tenth[:, 0:1],
                                                               ALU.mult, ALU.add), c_pool)
            yield

        def valid(b):
            return 0 <= b < N

        def take(gen, n):
            for _ in range(n):
                if next(gen, "end") == "end":
                    return False
            return True

        def nothing():
            return
            yield

        for b in range(-2, N + 2):
            kept = {}
            if valid(b - 1) and (b - 1) not in loaded:
                load_x(b - 1)

            def background(b=b, kept=kept):
                if valid(b - 2) and b < N:
                    yield from pause(3)
                    yield from finish(b - 2, y_sb, [st["y"]])
                if valid(b - 1) and b < N:
                    yield from divide_heads(b - 1, 1)
                    yield from project_out(b - 1)
                    yield from pause(3)
                    yield from transpose_state(b - 1)
                if valid(b + 2):
                    kept["qk"] = yield from project_qk(b + 2)

            back = background()
            if valid(b):
                pieces, first_half = 0, 3 * (NG * NT + 2)
                for _ in attention_steps(b):
                    pieces += 1
                    take_maxima(pace(b, pieces))
                    if not take(back, 1) and pieces > first_half and (b, 0) not in divided:
                        back = divide_heads(b, 0)
                        take(back, 1)
                take(back, 1000)
                if (b, 0) not in divided:
                    take(divide_heads(b, 0), 1000)
            elif b < 0:
                for n in range(1000):
                    if not take(back, 1):
                        break
                    take_maxima(1)
                    if b == -2 and n == NT:
                        set_rows()
                if b == -2:
                    derive_constants()
            values = nothing()
            if valid(b + 2):
                lay_rows(b + 2, kept["qk"][1], main_end.get(b))
                values = project_v(b + 2, kept["qk"][0], main_end.get(b))

            late = nothing()
            if b == N - 1:
                load_x(N - 1)
                st.update({MAX[0]: reduced[0], MAX[1]: reduced[1], HEADS: heads_free[0]})
                rotation[:] = [MISC, *MAX, HEADS]

                def late_out():
                    yield from divide_heads(N - 1, 1)
                    yield from project_out(N - 1)
                late = late_out()
            elif b == N:
                for last in range(max(0, N - 2), N - 1):
                    late = finish(last, x_in, [*st["mom"][0], *st["mom"][1]])
                    take(late, 2 * NT // 2)
                take(transpose_state(N - 1), 1000)
            elif b == N + 1:
                first, second = (finish(N - 1, x_in, [st["y"]], range(h * TPH, (h + 1) * TPH)) for h in range(NH))
                take(first, TPH)
                while take(second, 1) | take(first, 1):
                    pass
            if valid(b - 1):
                for n, room in enumerate(coupling(b - 1)):
                    take_maxima(room)
                    take(late, 2)
                    if n % 8 == 7:
                        take(values, 1)
            take(values, 1000)
            take(late, 1000)

        for b in range(max(0, N - XS), N):
            sp.wait(stored[b])

        block = ctx.enter_context(nc.Block())
        for register, queue in ((block.sync, sp), (block.tensor, pe), (block.scalar, act), (block.vector, dve),
                                (block.gpsimd, pool)):
            @register
            def _(e, queue=queue):
                for f in queue.items:
                    f(e)


def kernel(**inputs):
    import numpy as np
    import concourse.bacc as bacc
    from concourse.bass_utils import run_bass_kernel_spmd

    arr = {k: np.asarray(v) for k, v in inputs.items()}
    by_side = lambda w: np.ascontiguousarray(w.reshape(8, 2, 8, 128).transpose(3, 1, 2, 0).reshape(128, 128))
    given = {
        "x": arr["L0_attn_x"],
        "wq_t": by_side(arr["L0_attn_Wq"]), "wk_t": by_side(arr["L0_attn_Wk"]),
        "wv_t": np.ascontiguousarray(arr["L0_attn_Wv"].T), "wo_t": np.ascontiguousarray(arr["L0_attn_Wo"].T),
        "bo": arr["L0_attn_bo"],
        "w1": arr["L0_ffn_cn_w1"], "b1": arr["L0_ffn_cn_b1"], "w2": arr["L0_ffn_cn_w2"], "b2": arr["L0_ffn_cn_b2"],
        "w3": arr["L0_ffn_cn_w3"], "b3": arr["L0_ffn_cn_b3"], "w4": arr["L0_ffn_cn_w4"], "b4": arr["L0_ffn_cn_b4"],
        "g1": arr["L0_ffn_gc_w1"], "gb1": arr["L0_ffn_gc_b1"], "g2": arr["L0_ffn_gc_w2"], "gb2": arr["L0_ffn_gc_b2"],
        "g3": arr["L0_ffn_gc_w3"], "gb3": arr["L0_ffn_gc_b3"], "ar": arr["L0_ffn_adaptive_range"],
    }
    nc = bacc.Bacc("TRN2", target_bir_lowering=False, num_devices=1)
    arrays, aps = {}, {}
    for name, v in given.items():
        v = np.ascontiguousarray(v)
        arrays[f"in_{name}"] = v
        aps[name] = nc.dram_tensor(f"in_{name}", v.shape, mybir.dt.from_np(v.dtype), kind="ExternalInput").ap()
    aps["out"] = nc.dram_tensor("out", given["x"].shape, F32, kind="ExternalOutput").ap()
    attention_ffn_program(nc, aps)
    r = run_bass_kernel_spmd(nc, [arrays], core_ids=[0])
    return r.results[0]["out"]
```
